# Optimizing a Trainium2 kernel written in Bass

```python
import numpy as np
import jax
import jax.numpy as jnp

def _softmax(x, axis=-1):
    return jax.nn.softmax(x, axis=axis)

def _gelu(x):
    return jax.nn.gelu(x, approximate=True)

def _silu(x):
    return jax.nn.silu(x)

def _sigmoid(x):
    return jax.nn.sigmoid(x)

def _layernorm(x, axis=-1, eps=1e-05):
    m = jnp.mean(x, axis=axis, keepdims=True)
    v = jnp.var(x, axis=axis, keepdims=True)
    return (x - m) / jnp.sqrt(v + eps)

def _scatter_add(tgt, idx, src, axis=0):
    return tgt.at[idx].add(src)

def _segment_sum(src, seg, n):
    return jax.ops.segment_sum(src, seg, n)
kernel_name = 'mk_hybrid_d1_jaxref_r8_1e54bb'

def setup_inputs(seed: int=0):
    np.random.seed(seed)
    _w = jnp.asarray

    def _L0_attn_a_setup():
        import jax, jax.numpy as jnp
        import numpy as np
        N_HEAD = 16
        LATENT = 32

        def _rotate_half(x):
            xe = x[..., ::2]
            xo = x[..., 1::2]
            return jnp.stack((-xo, xe), axis=-1).reshape(x.shape)

        def _rope_tables(T, latent_dim, dtype):
            inv_freq = 1.0 / 10000.0 ** (jnp.arange(0, latent_dim, 2, dtype=jnp.float32) / latent_dim)
            t = jnp.arange(T, dtype=jnp.float32)
            freqs = jnp.outer(t, inv_freq)
            cos = jnp.repeat(jnp.cos(freqs), 2, axis=-1)[:, :latent_dim]
            sin = jnp.repeat(jnp.sin(freqs), 2, axis=-1)[:, :latent_dim]
            return (cos.astype(dtype), sin.astype(dtype))
        key = jax.random.key(seed)
        ks = jax.random.split(key, 14)
        C = 128
        hd = C // N_HEAD
        L = LATENT
        s = 0.02
        return {'x': jax.random.normal(ks[0], (4, 256, C), jnp.float32), 'c_attn_w': jax.random.normal(ks[1], (3 * C, C), jnp.float32) * s, 'c_attn_b': jnp.zeros((3 * C,), jnp.float32), 'q2l_w': jax.random.normal(ks[2], (L, hd), jnp.float32) * s, 'q2l_b': jnp.zeros((L,), jnp.float32), 'kv2l_w': jax.random.normal(ks[3], (L, hd), jnp.float32) * s, 'kv2l_b': jnp.zeros((L,), jnp.float32), 'l2o_w': jax.random.normal(ks[4], (hd, L), jnp.float32) * s, 'l2o_b': jnp.zeros((hd,), jnp.float32), 'wqk_w': jax.random.normal(ks[5], (L, L), jnp.float32) * s, 'wqk_b': jnp.zeros((L,), jnp.float32), 'cproj_w': jax.random.normal(ks[6], (C, C), jnp.float32) * s, 'cproj_b': jnp.zeros((C,), jnp.float32)}
    _L0_attn_a_in = _L0_attn_a_setup()

    def _L0_attn_b_setup():
        import jax, jax.numpy as jnp
        import numpy as np
        D_MODEL = 128
        NUM_HEADS = 16
        D_K = D_MODEL // NUM_HEADS
        B, S = (4, 256)
        key = jax.random.key(seed)
        k1, k2, k3 = jax.random.split(key, 3)
        x = jax.random.normal(k1, (B, S, D_MODEL), dtype=jnp.float32)
        w_qkv = jax.random.normal(k2, (3, NUM_HEADS, D_K, D_MODEL), dtype=jnp.float32) / np.sqrt(D_MODEL)
        w_o = jax.random.normal(k3, (D_MODEL, D_MODEL), dtype=jnp.float32) / np.sqrt(D_MODEL)
        return {'x': x, 'w_qkv': w_qkv, 'w_o': w_o}
    _L0_attn_b_in = _L0_attn_b_setup()

    def _L0_ffn_setup():
        import jax, jax.numpy as jnp
        import numpy as np
        B, S, D, H, F, E = (2, 128, 128, 16, 512, 8)
        HD = D // H
        EPS = 1e-06

        def _layernorm(x, g, b):
            m = jnp.mean(x, axis=-1, keepdims=True)
            v = jnp.var(x, axis=-1, keepdims=True)
            return (x - m) / jnp.sqrt(v + EPS) * g + b
        key = jax.random.key(seed)
        ks = jax.random.split(key, 10)
        sc = 0.02
        x = jax.random.normal(ks[0], (B, S, D), jnp.float32)
        Wq = jax.random.normal(ks[1], (D, D), jnp.float32) * sc
        Wk = jax.random.normal(ks[2], (D, D), jnp.float32) * sc
        Wv = jax.random.normal(ks[3], (D, D), jnp.float32) * sc
        Wo = jax.random.normal(ks[4], (D, D), jnp.float32) * sc
        bo = jnp.zeros((D,), jnp.float32)
        Wr = jax.random.normal(ks[5], (D, E), jnp.float32) * sc
        We1 = jax.random.normal(ks[6], (E, D, F), jnp.float32) * sc
        be1 = jnp.zeros((E, F), jnp.float32)
        We2 = jax.random.normal(ks[7], (E, F, D), jnp.float32) * sc
        be2 = jnp.zeros((E, D), jnp.float32)
        ln1_g = jnp.ones((D,), jnp.float32)
        ln1_b = jnp.zeros((D,), jnp.float32)
        ln2_g = jnp.ones((D,), jnp.float32)
        ln2_b = jnp.zeros((D,), jnp.float32)
        return {'x': x, 'Wq': Wq, 'Wk': Wk, 'Wv': Wv, 'Wo': Wo, 'bo': bo, 'Wr': Wr, 'We1': We1, 'be1': be1, 'We2': We2, 'be2': be2, 'ln1_g': ln1_g, 'ln1_b': ln1_b, 'ln2_g': ln2_g, 'ln2_b': ln2_b}
    _L0_ffn_in = _L0_ffn_setup()
    _d = {'L0_attn_a_x': _L0_attn_a_in['x'], 'L0_attn_a_c_attn_w': _L0_attn_a_in['c_attn_w'], 'L0_attn_a_c_attn_b': _L0_attn_a_in['c_attn_b'], 'L0_attn_a_q2l_w': _L0_attn_a_in['q2l_w'], 'L0_attn_a_q2l_b': _L0_attn_a_in['q2l_b'], 'L0_attn_a_kv2l_w': _L0_attn_a_in['kv2l_w'], 'L0_attn_a_kv2l_b': _L0_attn_a_in['kv2l_b'], 'L0_attn_a_l2o_w': _L0_attn_a_in['l2o_w'], 'L0_attn_a_l2o_b': _L0_attn_a_in['l2o_b'], 'L0_attn_a_wqk_w': _L0_attn_a_in['wqk_w'], 'L0_attn_a_wqk_b': _L0_attn_a_in['wqk_b'], 'L0_attn_a_cproj_w': _L0_attn_a_in['cproj_w'], 'L0_attn_a_cproj_b': _L0_attn_a_in['cproj_b'], 'L0_attn_b_w_qkv': _L0_attn_b_in['w_qkv'], 'L0_attn_b_w_o': _L0_attn_b_in['w_o'], 'L0_ffn_Wq': _L0_ffn_in['Wq'], 'L0_ffn_Wk': _L0_ffn_in['Wk'], 'L0_ffn_Wv': _L0_ffn_in['Wv'], 'L0_ffn_Wo': _L0_ffn_in['Wo'], 'L0_ffn_bo': _L0_ffn_in['bo'], 'L0_ffn_Wr': _L0_ffn_in['Wr'], 'L0_ffn_We1': _L0_ffn_in['We1'], 'L0_ffn_be1': _L0_ffn_in['be1'], 'L0_ffn_We2': _L0_ffn_in['We2'], 'L0_ffn_be2': _L0_ffn_in['be2'], 'L0_ffn_ln1_g': _L0_ffn_in['ln1_g'], 'L0_ffn_ln1_b': _L0_ffn_in['ln1_b'], 'L0_ffn_ln2_g': _L0_ffn_in['ln2_g'], 'L0_ffn_ln2_b': _L0_ffn_in['ln2_b']}
    _x0 = _d['L0_attn_a_x']
    _d['L0_attn_a_x'] = jax.random.normal(jax.random.fold_in(jax.random.key(seed), 1), (4, 512, 128), dtype=_x0.dtype)
    del _x0
    return _d

def reference(L0_attn_a_x, L0_attn_a_c_attn_w, L0_attn_a_c_attn_b, L0_attn_a_q2l_w, L0_attn_a_q2l_b, L0_attn_a_kv2l_w, L0_attn_a_kv2l_b, L0_attn_a_l2o_w, L0_attn_a_l2o_b, L0_attn_a_wqk_w, L0_attn_a_wqk_b, L0_attn_a_cproj_w, L0_attn_a_cproj_b, L0_attn_b_w_qkv, L0_attn_b_w_o, L0_ffn_Wq, L0_ffn_Wk, L0_ffn_Wv, L0_ffn_Wo, L0_ffn_bo, L0_ffn_Wr, L0_ffn_We1, L0_ffn_be1, L0_ffn_We2, L0_ffn_be2, L0_ffn_ln1_g, L0_ffn_ln1_b, L0_ffn_ln2_g, L0_ffn_ln2_b):

    def _L0_attn_a_ref(x, c_attn_w, c_attn_b, q2l_w, q2l_b, kv2l_w, kv2l_b, l2o_w, l2o_b, wqk_w, wqk_b, cproj_w, cproj_b):
        import jax, jax.numpy as jnp
        import numpy as np
        N_HEAD = 16
        LATENT = 32

        def _rotate_half(x):
            xe = x[..., ::2]
            xo = x[..., 1::2]
            return jnp.stack((-xo, xe), axis=-1).reshape(x.shape)

        def _rope_tables(T, latent_dim, dtype):
            inv_freq = 1.0 / 10000.0 ** (jnp.arange(0, latent_dim, 2, dtype=jnp.float32) / latent_dim)
            t = jnp.arange(T, dtype=jnp.float32)
            freqs = jnp.outer(t, inv_freq)
            cos = jnp.repeat(jnp.cos(freqs), 2, axis=-1)[:, :latent_dim]
            sin = jnp.repeat(jnp.sin(freqs), 2, axis=-1)[:, :latent_dim]
            return (cos.astype(dtype), sin.astype(dtype))
        B, T, C = x.shape
        H = N_HEAD
        hd = C // H
        L = q2l_w.shape[0]
        qkv = x @ c_attn_w.T + c_attn_b
        q, k, v = jnp.split(qkv, 3, axis=2)

        def heads(t):
            return t.reshape(B, T, H, hd).transpose(0, 2, 1, 3)
        q, k, v = (heads(q), heads(k), heads(v))
        q_lat = q @ q2l_w.T + q2l_b
        k_lat = k @ kv2l_w.T + kv2l_b
        v_lat = v @ kv2l_w.T + kv2l_b
        cos, sin = _rope_tables(T, L, x.dtype)
        cos = cos[None, None]
        sin = sin[None, None]
        q_lat = q_lat * cos + _rotate_half(q_lat) * sin
        k_lat = k_lat * cos + _rotate_half(k_lat) * sin
        q_for_k = q_lat @ wqk_w.T + wqk_b
        att = jnp.einsum('bhql,bhkl->bhqk', q_for_k, k_lat) * L ** (-0.5)
        causal = jnp.tril(jnp.ones((T, T), dtype=bool))
        att = jnp.where(causal[None, None], att, -jnp.inf)
        att = jax.nn.softmax(att, axis=-1)
        y_lat = jnp.einsum('bhqk,bhkl->bhql', att, v_lat)
        y = y_lat @ l2o_w.T + l2o_b
        y = y.transpose(0, 2, 1, 3).reshape(B, T, C)
        return y @ cproj_w.T + cproj_b

    def _L0_attn_b_ref(x, w_qkv, w_o):
        import jax, jax.numpy as jnp
        import numpy as np
        D_MODEL = 128
        NUM_HEADS = 16
        D_K = D_MODEL // NUM_HEADS
        B, S = (4, 256)
        seq_len = x.shape[-2]
        d_k = w_qkv.shape[-2]
        qkv = jnp.einsum('bsm,qhkm->qbhsk', x, w_qkv)
        Q, K, V = (qkv[0], qkv[1], qkv[2])
        scores = jnp.einsum('bhsk,bhtk->bhst', Q, K) / jnp.sqrt(jnp.asarray(d_k, x.dtype))
        causal = jnp.tril(jnp.ones((seq_len, seq_len), dtype=bool))
        scores = jnp.where(causal, scores, -jnp.inf)
        probs = jax.nn.softmax(scores, axis=-1)
        attn = jnp.einsum('bhst,bhtk->bhsk', probs, V)
        b, h, s, k = attn.shape
        attn_cat = jnp.transpose(attn, (0, 2, 1, 3)).reshape(b, s, h * k)
        return jnp.einsum('bsd,md->bsm', attn_cat, w_o)

    def _L0_ffn_ref(x, Wq, Wk, Wv, Wo, bo, Wr, We1, be1, We2, be2, ln1_g, ln1_b, ln2_g, ln2_b):
        import jax, jax.numpy as jnp
        import numpy as np
        B, S, D, H, F, E = (2, 128, 128, 16, 512, 8)
        HD = D // H
        EPS = 1e-06

        def _layernorm(x, g, b):
            m = jnp.mean(x, axis=-1, keepdims=True)
            v = jnp.var(x, axis=-1, keepdims=True)
            return (x - m) / jnp.sqrt(v + EPS) * g + b
        b, s, d = x.shape

        def split_heads(t):
            return t.reshape(b, s, H, HD).transpose(0, 2, 1, 3)
        q = split_heads(x @ Wq)
        k = split_heads(x @ Wk)
        v = split_heads(x @ Wv)
        scores = jnp.einsum('bhqd,bhkd->bhqk', q, k) / jnp.sqrt(jnp.float32(HD))
        attn_w = jax.nn.softmax(scores, axis=-1)
        ctx = jnp.einsum('bhqk,bhkd->bhqd', attn_w, v)
        ctx = ctx.transpose(0, 2, 1, 3).reshape(b, s, d)
        attn_out = ctx @ Wo + bo
        out1 = _layernorm(x + attn_out, ln1_g, ln1_b)
        router_probs = jax.nn.softmax(out1 @ Wr, axis=-1)
        top_g, top_i = jax.lax.top_k(router_probs, 2)
        top_g = jax.nn.softmax(top_g, axis=-1)
        acc = jnp.zeros_like(out1)
        for e in range(E):
            sel = top_i == e
            msk = jnp.any(sel, axis=-1)[..., None].astype(out1.dtype)
            h = jax.nn.gelu(out1 * msk @ We1[e] + be1[e], approximate=False)
            o = h @ We2[e] + be2[e]
            gate = jnp.sum(top_g * sel.astype(top_g.dtype), axis=-1, keepdims=True)
            acc = acc + o * gate
        return _layernorm(out1 + acc, ln2_g, ln2_b)
    x = L0_attn_a_x
    x = x + _L0_attn_a_ref(_layernorm(x, axis=-1), L0_attn_a_c_attn_w, L0_attn_a_c_attn_b, L0_attn_a_q2l_w, L0_attn_a_q2l_b, L0_attn_a_kv2l_w, L0_attn_a_kv2l_b, L0_attn_a_l2o_w, L0_attn_a_l2o_b, L0_attn_a_wqk_w, L0_attn_a_wqk_b, L0_attn_a_cproj_w, L0_attn_a_cproj_b)
    x = x + _L0_ffn_ref(_layernorm(x, axis=-1), L0_ffn_Wq, L0_ffn_Wk, L0_ffn_Wv, L0_ffn_Wo, L0_ffn_bo, L0_ffn_Wr, L0_ffn_We1, L0_ffn_be1, L0_ffn_We2, L0_ffn_be2, L0_ffn_ln1_g, L0_ffn_ln1_b, L0_ffn_ln2_g, L0_ffn_ln2_b)
    x = x + _L0_attn_b_ref(_layernorm(x, axis=-1), L0_attn_b_w_qkv, L0_attn_b_w_o)
    x = x + _L0_ffn_ref(_layernorm(x, axis=-1), L0_ffn_Wq, L0_ffn_Wk, L0_ffn_Wv, L0_ffn_Wo, L0_ffn_bo, L0_ffn_Wr, L0_ffn_We1, L0_ffn_be1, L0_ffn_We2, L0_ffn_be2, L0_ffn_ln1_g, L0_ffn_ln1_b, L0_ffn_ln2_g, L0_ffn_ln2_b)
    return x

_drawn_inputs = setup_inputs


def setup_inputs(seed=0):
    import zlib

    import numpy as np

    out = dict(_drawn_inputs(seed))
    spreads = {'L0_attn_a_c_attn_b': (0.0, 0.8),
     'L0_attn_a_q2l_b': (0.0, 0.8),
     'L0_attn_a_kv2l_b': (0.0, 0.8),
     'L0_attn_a_l2o_b': (0.0, 0.304),
     'L0_attn_a_wqk_b': (0.0, 0.8),
     'L0_attn_a_cproj_b': (0.0, 0.1),
     'L0_ffn_bo': (0.0, 0.1),
     'L0_ffn_be1': (0.0, 0.599),
     'L0_ffn_be2': (0.0, 0.1),
     'L0_ffn_ln1_g': (1.0, 0.2),
     'L0_ffn_ln1_b': (0.0, 0.1),
     'L0_ffn_ln2_g': (1.0, 0.2),
     'L0_ffn_ln2_b': (0.0, 0.1)}
    factors = {'L0_attn_a_c_attn_w': 8.0,
     'L0_attn_a_q2l_w': 8.0,
     'L0_attn_a_kv2l_w': 8.0,
     'L0_attn_a_l2o_w': 8.0,
     'L0_attn_a_wqk_w': 8.0,
     'L0_ffn_Wq': 8.0,
     'L0_ffn_Wk': 8.0,
     'L0_ffn_Wv': 8.0,
     'L0_ffn_Wo': 8.0}
    for name, (base, spread) in spreads.items():
        noise = np.random.default_rng([zlib.crc32(name.encode()), seed]).standard_normal(out[name].shape)
        drawn = base * np.exp(spread * noise) if base else spread * noise
        out[name] = jnp.asarray(drawn.astype(out[name].dtype))
    for name, factor in factors.items():
        out[name] = (out[name] * factor).astype(out[name].dtype)
    return out
```

```python
from contextlib import ExitStack

import numpy as np

import concourse.bass as bass
from concourse import mybir
from concourse.alu_op_type import AluOpType as ALU

ACT = mybir.ActivationFunctionType
AX = mybir.AxisListType
F32 = mybir.dt.float32
F32R = mybir.dt.float32r
BF16 = mybir.dt.bfloat16
U32 = mybir.dt.uint32

P = 128
T = 512
QT = T // P
H = 16
HD = 8
LAT = 32
GH = 4
NG = H // GH
E = 8
FC = 4
NEG = -1e30
LAYERS = ("latent", "ffn", "causal", "ffn")
M_ROW = 24
M_ROW_LAT = 96


def constants():
    cols, at, n = [], {}, 0

    def put(name, a):
        nonlocal n
        full = np.zeros((P, a.shape[1]), np.float32)
        full[: a.shape[0]] = a
        cols.append(full)
        at[name] = (n, n + a.shape[1])
        n += a.shape[1]

    eye = np.eye(P, dtype=np.float32)
    i = np.arange(P)
    put("ident", eye)
    put("mask_qk", np.where(i[None, :] > i[:, None], np.float32(NEG), np.float32(0)))
    put("mask_kq", np.where(i[:, None] > i[None, :], np.float32(NEG), np.float32(0)))
    exponent = np.arange(0, LAT, 2, dtype=np.float32) / np.float32(LAT)
    inv = (np.float32(1.0) / np.power(np.float32(10000.0), exponent)).astype(np.float32)
    freqs = np.outer(np.arange(T, dtype=np.float32), inv).astype(np.float32)
    cos = np.repeat(np.cos(freqs), 2, axis=1).T.astype(np.float32)
    sin = np.repeat(np.sin(freqs), 2, axis=1).T.astype(np.float32)
    put("cos_sin", np.concatenate([cos, sin, cos, sin]))
    put("own_head", (i[:, None] // HD == np.arange(H)[None, :]).astype(np.float32))
    i32 = np.eye(LAT, dtype=np.float32)
    rot_t = np.zeros((LAT, LAT), np.float32)
    for k in range(0, LAT, 2):
        rot_t[k + 1, k] = -1.0
        rot_t[k, k + 1] = 1.0
    put("sum3", np.tile(np.concatenate([i32, i32, i32, np.zeros_like(i32)], 1), (4, 1)))
    s = i % 32
    put("q_low", ((s >= 8) & (s < 16)).astype(np.float32)[:, None])
    put("k_low", ((s >= 16) & (s < 24)).astype(np.float32)[:, None])
    put("k_one", ((s == M_ROW) | (s == M_ROW + 1)).astype(np.float32)[:, None])
    put("lq_low", ((i >= 32) & (i < 64)).astype(np.float32)[:, None])
    put("lk_low", ((i >= 64) & (i < 96)).astype(np.float32)[:, None])
    put("lk_one", np.stack([(i - M_ROW_LAT) // 2 == j for j in range(GH)], 1).astype(np.float32))
    put("zero", np.zeros((P, 1), np.float32))
    put("expert", np.tile(np.arange(E, dtype=np.float32)[None], (P, 1)))
    put("neg_half", np.full((P, QT), -0.5, np.float32))
    put("eye_rot", np.concatenate([i32, rot_t], 1))
    put("eye_rot2", np.concatenate([i32, rot_t, i32, rot_t], 1))
    put("eye4", np.tile(i32, (1, 4)))
    return np.concatenate(cols, 1), at


CONST, CONST_AT = constants()


def events():
    misc, scores, smax = {}, {}, {}

    def add(ring, *name):
        ring[name] = len(ring)

    for L, kind in enumerate(LAYERS):
        for n in ("yT", "v"):
            add(misc, n, L)
        for act in schedule(kind):
            what, g = act[0], act[1]
            if what == "proj" and kind == "latent":
                pr = act[2]
                for n in ("m1q", "m1k"):
                    add(misc, n, L, g, pr)
                for j in (2 * pr, 2 * pr + 1):
                    for n in ("m2q", "m2k"):
                        add(misc, n, L, g, j)
            elif what == "proj":
                add(misc, "pq", L, g)
                add(misc, "pk", L, g)
            elif what == "max":
                for qt in range(QT):
                    add(smax, "s", L, g, act[2], qt)
            elif what == "maxT":
                add(misc, "mT", L, g)
            elif what == "st":
                for kt in range(QT):
                    add(scores, "st", L, g, act[2], kt)
            elif what == "oT":
                add(misc, "oT", L, g)
        add(misc, "cT", L)
        add(misc, "wo", L)
        if kind == "ffn":
            for n in ("zT", "rt", "gT", "be2"):
                add(misc, n, L)
            for e in range(E):
                for c in range(FC):
                    add(scores, "h", L, e, c)
                add(smax, "o", L, e)
    return misc, scores, smax


def schedule(kind):
    latent = kind == "latent"
    acts = [("proj", 0, pr) for pr in range(GH // 2)] if latent else [("proj", 0)]
    for t in range(NG + 2):
        for j in range(GH):
            if t < NG:
                acts.append(("max", t, j))
            if j == 0 and 1 <= t <= NG:
                acts.append(("maxT", t - 1))
            if 1 <= t <= NG:
                acts.append(("st", t - 1, j))
            if j == 0 and t >= 2:
                acts.append(("av", t - 2))
            if t + 1 < NG and latent and j % 2:
                acts.append(("proj", t + 1, j // 2))
            if t + 1 < NG and not latent and j == 1:
                acts.append(("proj", t + 1))
            if j == 2 and t >= 2:
                acts.append(("oT", t - 2))
    return acts


MISC, SCORES, SMAX = events()


def hybrid_kernel(nc, x, wa, ba, q2l, q2lb, kv2l, kv2lb, l2o, l2ob, wqk, wqkb, cproj, cprojb,
                  wqkv, wo_b, wq, wk, wv, wo, bo, wr, we1, be1, we2, be2, g1, b1, g2, b2, const, out):
    with ExitStack() as ctx:
        def sb(name, shape, dt=F32):
            return ctx.enter_context(nc.sbuf_tensor(name, shape, dt))

        def sem(name):
            return ctx.enter_context(nc.semaphore(name))

        ps = ctx.enter_context(nc.psum_tensor("ps", [P, 8, T], F32))
        SM_BANK, ST_BANK, X_BANK, O_BANK = (0, 1), (2, 3, 4), (5, 6), 7

        cst = sb("cst", [P, CONST.shape[1]])
        ident_bf = sb("ident_bf", [P, P], BF16)
        mask_bf = sb("mask_bf", [P, 2, P], BF16)
        small = sb("small", [P, 128])
        wrep = sb("wrep", [P, 4, NG, P])
        w_v = sb("w_v", [P, 3, P])
        w_o = sb("w_o", [P, 3, P])
        cprojT = sb("cprojT", [P, P])
        w_lat = sb("w_lat", [P, 2, H, 2 * LAT])
        b_lat = sb("b_lat", [P, 2, H // 2])
        w_m2q = sb("w_m2q", [P, P])
        bq_m2 = sb("bq_m2", [P, 1])
        bq_m2_low = sb("bq_m2_low", [P, 1])
        bcast = sb("bcast", [P, 2, P])
        cvec = sb("cvec", [P, 1])
        bias_lat = sb("bias_lat", [P, P])
        rows = sb("rows", [P, 6, P])
        wr_sb = sb("wr_sb", [P, E])
        we1_sb = sb("we1_sb", [P, E, FC * P])
        we2_sb = sb("we2_sb", [P, E, FC, P])
        be1_sb = sb("be1_sb", [P, E * FC])
        be2_sb = sb("be2_sb", [P, P])
        xs = sb("xs", [P, QT, P])
        ys = sb("ys", [P, QT, P])
        yT = sb("yT", [P, T])
        va = sb("va", [P, QT, H, 32])
        q_part = sb("q_part", [P, T], F32R)
        k_part = sb("k_part", [P, T], F32R)
        r1 = sb("r1", [P, 2, T])
        qs = sb("qs", [P, 2, GH, T], F32R)
        ks = sb("ks", [P, 2, GH, T], F32R)
        nmax = sb("nmax", [P, GH, QT])
        mx = sb("mx", [P, 2, QT, P], F32R)
        probs = sb("probs", [P, 2, GH, QT, T])
        os_ = sb("os_", [P, 2, T])
        rden = sb("rden", [P, QT, GH])
        ctxs = sb("ctxs", [P, QT, P])
        ctxT = sb("ctxT", [P, T])
        zs = sb("zs", [P, QT, P])
        zT = sb("zT", [P, T])
        acc = sb("acc", [P, QT, P])
        tmp = sb("tmp", [P, QT, P])
        hid = probs[:, 0]
        st6 = sb("st6", [P, QT, 6])
        mv = sb("mv", [P, QT, 2])
        vare = sb("vare", [P, QT])
        rstd = sb("rstd", [P, QT])
        lg = sb("lg", [P, 6, QT, E])
        lgi = sb("lgi", [P, QT, E], U32)
        lgf = sb("lgf", [P, QT, E])
        r4 = sb("r4", [P, 8, QT])
        gT = sb("gT", [P, T])

        raw = probs[:, 1, 0].rearrange("p t n -> p (t n)")[:, 0:9 * P].rearrange("p (m n) -> p m n", n=P)
        blockd = r1[:].rearrange("p m (h l) -> p (m h) l", l=2 * LAT)

        def c(name):
            a, b = CONST_AT[name]
            return cst[:, a:b]

        loaded = sem("loaded")
        prep_pe = sem("prep_pe")
        prep_dve = sem("prep_dve")

        with nc.Block() as block:
            n_loads = [0]

            @block.sync
            def _(sp):
                def load(dst, src):
                    n_loads[0] += 1
                    sp.dma_start(dst, src, allow_slow_non_contiguous=True).then_inc(loaded, 16)

                def every_partition(a, n, p=P):
                    return a.rearrange("(o n) -> o n", o=1).broadcast_to([p, n])

                load(cst[:], const)
                load(raw[:, 0:3, :], wa.rearrange("(s o) d -> o s d", s=3))
                load(raw[:, 3, :], cproj)
                load(raw[:, 4:7, :], wqkv.rearrange("s h k m -> (h k) s m"))
                load(raw[:, 7, :], wo_b)
                load(small[:, 0:3], ba.rearrange("(s o) -> o s", s=3))
                load(small[0:LAT, 4:12], q2l)
                load(small[0:LAT, 12:20], kv2l)
                load(small[0:LAT, 20:21], q2lb.rearrange("(n o) -> n o", o=1))
                load(small[0:LAT, 21:22], kv2lb.rearrange("(n o) -> n o", o=1))
                load(small[0:LAT, 24:32], l2o.rearrange("o l -> l o"))
                load(small[0:LAT, 32:64], wqk.rearrange("o l -> l o"))
                for r in range(3):
                    load(small[r * LAT:(r + 1) * LAT, 64:65], wqkb.rearrange("(n o) -> n o", o=1))
                for h in range(H):
                    load(small[h * HD:(h + 1) * HD, 65:66], l2ob.rearrange("(n o) -> n o", o=1))
                load(raw[:, 8, :], wq)
                load(bcast[:, 0, :], wk)
                load(w_v[:, 1, :], wv)
                load(w_o[:, 1, :], wo)
                for r, a in enumerate((bo, g1, b1, g2, b2, cprojb)):
                    load(rows[:, r, :], every_partition(a, P))
                load(wr_sb[:], wr)
                load(be1_sb[:], be1.rearrange("e (c p) -> p (e c)", p=P))
                load(be2_sb[0:E, :], be2)
                load(we1_sb[:], we1.rearrange("e d f -> d e f"))
                load(we2_sb[:], we2.rearrange("e (c p) d -> p e c d", p=P))

            @block.vector
            def _(dve):
                done = [0]

                def step(ins):
                    done[0] += 1
                    ins.then_inc(prep_dve, 1)
                    dve.wait_ge(prep_dve, done[0])

                step(dve.memset(va[:], 1.0))
                step(dve.memset(w_m2q[:], 0.0))
                step(dve.memset(wrep[:], 0.0))
                step(dve.memset(bq_m2[:], 0.0))
                step(dve.memset(mx[:].bitcast(F32), 0.0))
                dve.wait_ge(loaded, 16 * n_loads[0])
                step(dve.tensor_copy(ident_bf[:], c("ident")))
                step(dve.tensor_copy(mask_bf[:, 0, :], c("mask_qk")))
                step(dve.tensor_copy(mask_bf[:, 1, :], c("mask_kq")))
                step(dve.tensor_copy(bq_m2[0:96, :], small[0:96, 64:65]))
                step(dve.tensor_tensor(bq_m2_low[:], bq_m2[:], c("lq_low"), ALU.mult))
                for n, col in enumerate((4, 12, 24)):
                    step(dve.tensor_copy(tmp[0:LAT, n, :].rearrange("p (h i) -> p h i", h=H),
                                         small[0:LAT, col:col + HD].unsqueeze(1).broadcast_to([LAT, H, HD])))
                for m, src in enumerate((raw[:, 8, :], bcast[:, 0, :])):
                    for r in range(3):
                        step(dve.tensor_copy(
                            wrep[:, m].rearrange("p g (j s) -> p (g j) s", j=GH)[:, :, 8 * r:8 * r + 8],
                            src.rearrange("p (h i) -> p h i", h=H)))
                ready = done[0]
                assert ready == PREP_REP
                dve.wait_ge(prep_pe, 1)
                step(dve.tensor_copy(w_v[:, 0, :], ps[:, 0, 0:P]))
                step(dve.tensor_copy(cprojT[:], ps[:, 0, P:2 * P]))
                for m in range(2):
                    for r in range(3):
                        step(dve.tensor_copy(
                            wrep[:, 2 + m].rearrange("p g (j s) -> p (g j) s", j=GH)[:, :, 8 * r:8 * r + 8],
                            ps[:, 0, (2 + m) * P:(3 + m) * P].rearrange("p (h i) -> p h i", h=H)))
                step(dve.tensor_copy(w_v[:, 2, :], ps[:, 1, 0:P]))
                step(dve.tensor_copy(w_o[:, 2, :], ps[:, 1, P:2 * P]))
                for m in range(2):
                    dve.wait_ge(prep_pe, 2 + 2 * m)
                    step(dve.tensor_tensor(
                        blockd, ps[:, 2, 64 * m:64 * m + 64].unsqueeze(1).broadcast_to([P, H, 64]),
                        c("own_head").unsqueeze(2).broadcast_to([P, H, 64]), ALU.mult))
                    dve.wait_ge(prep_pe, 3 + 2 * m)
                    step(dve.tensor_copy(w_lat[:, m].rearrange("p h l -> p (h l)"),
                                         ps[:, 3:5, :].rearrange("p a b -> p (a b)")))
                    step(dve.tensor_copy(b_lat[:, m, :], ps[:, 5, 0:H // 2]))
                for r in range(3):
                    step(dve.tensor_copy(w_m2q[:, r * LAT:(r + 1) * LAT], ps[:, 2, 128:160]))
                step(dve.tensor_tensor(
                    bcast[:, 0, :].rearrange("p (h i) -> p h i", h=H),
                    ps[:, 2, 160:168].unsqueeze(1).broadcast_to([P, H, HD]),
                    c("own_head").unsqueeze(2).broadcast_to([P, H, HD]), ALU.mult))
                step(dve.tensor_tensor(cvec[:], ps[:, 2, 168:169], small[:, 65:66], ALU.add))
                step(dve.tensor_copy(bcast[:, 1, :], cvec[:, 0:1].broadcast_to([P, P])))
                dve.wait_ge(prep_pe, 6)
                step(dve.tensor_copy(w_o[:, 0, :], ps[:, 0, 0:P]))
                step(dve.tensor_copy(tmp[:, 3, :], small[:, 2:3].broadcast_to([P, P])))
                dve.wait_ge(prep_pe, 7)
                step(dve.tensor_tensor(bias_lat[:], ps[:, 1, 0:P], rows[:, 5, :], ALU.add))

            @block.tensor
            def _(pe):
                ident = c("ident")
                pe.wait_ge(loaded, 16 * n_loads[0])
                pe.transpose(ps[:, 0, 0:P], raw[:, 2, :], ident)
                pe.transpose(ps[:, 0, P:2 * P], raw[:, 3, :], ident)
                pe.transpose(ps[:, 0, 2 * P:3 * P], raw[:, 4, :], ident)
                pe.transpose(ps[:, 0, 3 * P:4 * P], raw[:, 5, :], ident)
                pe.transpose(ps[:, 1, 0:P], raw[:, 6, :], ident)
                pe.transpose(ps[:, 1, P:2 * P], raw[:, 7, :], ident).then_inc(prep_pe, 1)
                pe.wait_ge(prep_dve, PREP_REP)
                pe.matmul(ps[:, 2, 0:64], tmp[0:LAT, 0, :], c("eye_rot")[0:LAT], start=True, stop=True,
                          skip_group_check=True)
                pe.matmul(ps[:, 2, 64:128], tmp[0:LAT, 1, :], c("eye_rot")[0:LAT], start=True, stop=True,
                          skip_group_check=True)
                pe.matmul(ps[:, 2, 128:160], c("eye4")[0:LAT], small[0:LAT, 32:64], start=True, stop=True,
                          skip_group_check=True)
                pe.matmul(ps[:, 2, 160:168], tmp[0:LAT, 2, :], small[0:LAT, 12:20], start=True, stop=True,
                          skip_group_check=True)
                pe.matmul(ps[:, 2, 168:169], tmp[0:LAT, 2, :], small[0:LAT, 21:22], start=True, stop=True,
                          skip_group_check=True).then_inc(prep_pe, 1)
                for m in range(2):
                    pe.wait_ge(prep_dve, PREP_BLOCKD + 3 * m)
                    bd = blockd.rearrange("p h l -> p (h l)")
                    for half in range(2):
                        pe.matmul(ps[:, 3 + half, :], raw[:, m, :], bd[:, half * T:(half + 1) * T],
                                  start=True, stop=True)
                    for pair in range(H // 2):
                        pe.matmul(ps[:, 5, pair:pair + 1], bd[:, pair * P:(pair + 1) * P], small[:, m:m + 1],
                                  start=True, stop=False, skip_group_check=True)
                        ins = pe.matmul(ps[:, 5, pair:pair + 1], c("eye_rot2")[0:LAT],
                                        small[0:LAT, 20 + m:21 + m], start=False, stop=True,
                                        skip_group_check=True)
                    ins.then_inc(prep_pe, 1)
                    if m == 0:
                        pe.matmul(ps[:, 6, 0:64], tmp[0:LAT, 1, :], c("eye_rot")[0:LAT], start=True,
                                  stop=True).then_inc(prep_pe, 1)
                pe.wait_ge(prep_dve, PREP_OUT)
                pe.matmul(ps[:, 0, 0:P], bcast[:, 0, :], cprojT[:], start=True, stop=True).then_inc(prep_pe, 1)
                pe.wait_ge(prep_dve, PREP_OUT + 2)
                pe.matmul(ps[:, 1, 0:P], bcast[:, 1, :], cprojT[:], start=True, stop=False)
                pe.matmul(ps[:, 1, 0:P], tmp[:, 3, :], w_o[:, 0, :], start=False, stop=True).then_inc(prep_pe, 1)

        x_in = sem("x_in")
        misc_full = sem("misc_full")
        misc_free = sem("misc_free")
        st_full = sem("st_full")
        st_free = sem("st_free")
        sm_full = sem("sm_full")
        sm_free = sem("sm_free")
        o_full = sem("o_full")
        o_free = sem("o_free")
        parts = sem("parts")
        split = sem("split")
        maxima = sem("maxima")
        shifted = sem("shifted")
        y_ready = sem("y_ready")
        yT_ready = sem("yT_ready")
        v_ready = sem("v_ready")
        r1_ready = sem("r1_ready")
        ctx_ready = sem("ctx_ready")
        ctxT_ready = sem("ctxT_ready")
        z_ready = sem("z_ready")
        zT_ready = sem("zT_ready")
        logits = sem("logits")
        exped = sem("exped")
        gdiff = sem("gdiff")
        gates = sem("gates")
        gT_ready = sem("gT_ready")
        var_ready = sem("var_ready")
        rstd_ready = sem("rstd_ready")
        dve_step = sem("dve_step")
        pool_step = sem("pool_step")
        seq_done = sem("seq_done")
        stored = sem("stored")
        turn_sems = [x_in, misc_full, misc_free, st_full, st_free, sm_full, sm_free, o_full, o_free,
                     parts, split, maxima, shifted, y_ready, yT_ready, v_ready, r1_ready, ctx_ready,
                     ctxT_ready, z_ready, zT_ready, logits, exped, gdiff, gates, gT_ready,
                     var_ready, rstd_ready, dve_step, pool_step, seq_done, stored]

        xv = x.rearrange("b (t p) d -> b p t d", p=P)
        ov = out.rearrange("b (t p) d -> b p t d", p=P)
        FFN = {L: n for n, L in enumerate(i for i, k in enumerate(LAYERS) if k == "ffn")}

        def misc_bank(*name):
            return ps[:, X_BANK[MISC[name] % 2], :]

        def st_bank(*name):
            return ps[:, ST_BANK[SCORES[name] % 3], :]

        def sm_bank(*name):
            return ps[:, SM_BANK[SMAX[name] % 2], :]

        def splits(L, g):
            per = [2 * GH if k == "latent" else 2 for k in LAYERS]
            return NG * sum(per[:L]) + (g + 1) * per[L]

        def r1_uses(g, pr):
            return 2 * (2 * g + pr) + 2

        def operand(buf, L, g, j):
            if LAYERS[L] == "latent":
                return buf[:, g % 2, j, :]
            return buf[32 * j:32 * j + 32, g % 2, g // 2, :]

        with nc.Fori(0, x.shape[0]) as b:
            with nc.Block() as block:

                @block.sync
                def _(sp):
                    sp.dma_start(xs[:], xv[b]).then_inc(x_in, 16)
                    sp.wait_ge(seq_done, 1)
                    sp.dma_start(ov[b], xs[:]).then_inc(stored, 16)
                    sp.wait_ge(stored, 16)

                @block.gpsimd
                def _(pool):
                    n = 0
                    for kind in LAYERS:
                        for eps in (1e-5, 1e-6, 1e-6) if kind == "ffn" else (1e-5,):
                            pool.wait_ge(var_ready, n + 1)
                            pool.tensor_scalar(vare[:], mv[:, :, 1], eps, None, ALU.add).then_inc(pool_step, 1)
                            pool.wait_ge(pool_step, n + 1)
                            pool.tensor_tensor(rstd[:], vare[:], c("neg_half"), ALU.pow).then_inc(rstd_ready, 1)
                            n += 1

                @block.tensor
                def _(pe):
                    ident = c("ident")
                    ident_r = ident

                    def open_misc(*name):
                        if MISC[name] >= 2:
                            pe.wait_ge(misc_free, MISC[name] - 1)
                        return misc_bank(*name)

                    def open_st(*name):
                        if SCORES[name] >= 3:
                            pe.wait_ge(st_free, SCORES[name] - 2)
                        return st_bank(*name)

                    def open_sm(*name):
                        if SMAX[name] >= 2:
                            pe.wait_ge(sm_free, SMAX[name] - 1)
                        return sm_bank(*name)

                    def turn(src, *name):
                        bank = open_misc(*name)
                        for t in range(QT):
                            ins = pe.transpose(bank[:, t * P:(t + 1) * P], src(t), ident)
                        ins.then_inc(misc_full, 1)

                    def rows_out(lhs, w, *name):
                        bank = open_misc(*name)
                        n = w.shape[1]
                        for t in range(QT):
                            ins = pe.matmul(bank[:, t * n:(t + 1) * n], lhs[:, t * P:(t + 1) * P], w,
                                            start=True, stop=True, skip_group_check=True)
                        ins.then_inc(misc_full, 1)

                    def proj(L, g, pr=None):
                        kind = LAYERS[L]
                        if kind != "latent":
                            base = 0 if kind == "ffn" else 2
                            for m, n in enumerate(("pq", "pk")):
                                bank = open_misc(n, L, g)
                                pe.matmul(bank, wrep[:, base + m, g, :], yT[:], start=True, stop=True)\
                                    .then_inc(misc_full, 1)
                            return
                        for m, n in enumerate(("m1q", "m1k")):
                            bank = open_misc(n, L, g, pr)
                            h = GH * g + 2 * pr
                            pe.matmul(bank, w_lat[:, m, h:h + 2, :].rearrange("p h l -> p (h l)"), yT[:],
                                      start=True, stop=True).then_inc(misc_full, 1)
                        for j in (2 * pr, 2 * pr + 1):
                            lo = 64 * (j % 2)
                            for m, n in enumerate(("m2q", "m2k")):
                                bank = open_misc(n, L, g, j)
                                pe.wait_ge(r1_ready, r1_uses(g, pr) - 1 + m)
                                w = w_m2q[:] if m == 0 else c("sum3")
                                pe.matmul(bank, w[lo:lo + 64, :], r1[lo:lo + 64, m, :], start=True,
                                          stop=True).then_inc(misc_full, 1)

                    def maxima_scores(L, g, j):
                        kind = LAYERS[L]
                        pe.wait_ge(split, splits(L, g))
                        q, k = operand(qs, L, g, j), operand(ks, L, g, j)
                        if kind == "latent":
                            q, k = q[0:96], k[0:96]
                        for qt in range(QT):
                            bank = open_sm("s", L, g, j, qt)
                            n = T if kind == "ffn" else (qt + 1) * P
                            if kind != "ffn":
                                pe.matmul(bank[:, n - P:n], ident_bf[:], mask_bf[:, 0, :], start=True,
                                          stop=False, skip_group_check=True)
                            ins = pe.matmul(bank[:, 0:n], q[:, qt * P:(qt + 1) * P], k[:, 0:n],
                                            start=(kind == "ffn"), stop=True, skip_group_check=True)
                            ins.then_inc(sm_full, 1)

                    def key_scores(L, g, j):
                        kind = LAYERS[L]
                        pe.wait_ge(shifted, NG * L + g + 1)
                        q, k = operand(qs, L, g, j), operand(ks, L, g, j)
                        for kt in range(QT):
                            bank = open_st("st", L, g, j, kt)
                            lo = 0 if kind == "ffn" else kt * P
                            if kind != "ffn":
                                pe.matmul(bank[:, lo:lo + P], ident_bf[:], mask_bf[:, 1, :], start=True,
                                          stop=False, skip_group_check=True)
                            ins = pe.matmul(bank[:, lo:T], k[:, kt * P:(kt + 1) * P], q[:, lo:T],
                                            start=(kind == "ffn"), stop=True, skip_group_check=True)
                            ins.then_inc(st_full, 1)

                    def values(L, g):
                        kind = LAYERS[L]
                        pe.wait_ge(v_ready, L + 1)
                        pe.wait_ge(st_free, SCORES["st", L, g, GH - 1, QT - 1] + 1)
                        if NG * L + g > 0:
                            pe.wait_ge(o_free, NG * L + g)
                        for kt in reversed(range(QT)):
                            lo = 0 if kind == "ffn" else kt * P
                            for j in range(GH):
                                ins = pe.matmul(ps[32 * j:32 * j + 32, O_BANK, lo:T], va[:, kt, GH * g + j, :],
                                                probs[:, g % 2, j, kt, lo:T], start=(kt == QT - 1),
                                                stop=(kt == 0), skip_group_check=True)
                        ins.then_inc(o_full, 1)

                    for L, kind in enumerate(LAYERS):
                        wsel = {"latent": 0, "ffn": 1, "causal": 2}[kind]
                        pe.wait_ge(y_ready, L + 1)
                        turn(lambda t: ys[:, t, :], "yT", L)
                        pe.wait_ge(yT_ready, L + 1)
                        rows_out(yT, w_v[:, wsel, :], "v", L)
                        for act in schedule(kind):
                            g = act[1]
                            if act[0] == "proj":
                                proj(L, *act[1:])
                            elif act[0] == "max":
                                maxima_scores(L, g, act[2])
                            elif act[0] == "maxT":
                                pe.wait_ge(maxima, NG * L + g + 1)
                                turn(lambda t: mx[:, int(kind == "latent"), t, :].bitcast(F32), "mT", L, g)
                            elif act[0] == "st":
                                key_scores(L, g, act[2])
                            elif act[0] == "av":
                                values(L, g)
                            else:
                                pe.wait_ge(o_free, NG * L + g + 1)
                                turn(lambda t: os_[:, g % 2, t * P:(t + 1) * P], "oT", L, g)
                        pe.wait_ge(ctx_ready, L + 1)
                        turn(lambda t: ctxs[:, t, :], "cT", L)
                        pe.wait_ge(ctxT_ready, L + 1)
                        rows_out(ctxT, w_o[:, wsel, :], "wo", L)
                        if kind != "ffn":
                            continue
                        f = FFN[L]
                        pe.wait_ge(z_ready, f + 1)
                        turn(lambda t: zs[:, t, :], "zT", L)
                        pe.wait_ge(zT_ready, f + 1)
                        rows_out(zT, wr_sb[:], "rt", L)

                        def first(e):
                            for ch in range(FC):
                                bank = open_st("h", L, e, ch)
                                pe.matmul(bank, we1_sb[:, e, ch * P:(ch + 1) * P], zT[:], start=True,
                                          stop=True).then_inc(st_full, 1)

                        def second(e):
                            pe.wait_ge(st_free, SCORES["h", L, e, FC - 1] + 1)
                            bank = open_sm("o", L, e)
                            for t in range(QT):
                                for ch in range(FC):
                                    ins = pe.matmul(bank[:, t * P:(t + 1) * P],
                                                    hid[:, e % 2, ch, t * P:(t + 1) * P], we2_sb[:, e, ch, :],
                                                    start=(ch == 0), stop=(ch == FC - 1),
                                                    skip_group_check=True)
                            ins.then_inc(sm_full, 1)

                        first(0)
                        for e in range(E):
                            if e + 1 < E:
                                first(e + 1)
                            if e == 1:
                                pe.wait_ge(gates, f + 1)
                                bank = open_misc("gT", L)
                                for t in range(QT):
                                    ins = pe.transpose(bank[0:E, t * P:(t + 1) * P], lg[:, 5, t, :], ident)
                                ins.then_inc(misc_full, 1)
                                pe.wait_ge(gT_ready, f + 1)
                                bank = open_misc("be2", L)
                                for t in range(QT):
                                    ins = pe.matmul(bank[:, t * P:(t + 1) * P], gT[0:E, t * P:(t + 1) * P],
                                                    be2_sb[0:E, :], start=True, stop=True,
                                                    skip_group_check=True)
                                ins.then_inc(misc_full, 1)
                            second(e)

                @block.scalar
                def _(act):
                    def high_part(dst, L, name, scale, bias=None):
                        act.wait_ge(misc_full, MISC[name] + 1)
                        nonlocal n_parts
                        if n_parts >= 2:
                            act.wait_ge(split, n_parts - 1)
                        n_parts += 1
                        if bias is None:
                            ins = act.activation(dst[:], misc_bank(*name), ACT.Copy, scale=scale)
                        else:
                            ins = act.activation(dst[:], misc_bank(*name), ACT.Identity, scale=scale, bias=bias)
                        ins.then_inc(parts, 1)

                    n_parts = 0
                    for L, kind in enumerate(LAYERS):
                        scale = LAT ** -0.5 if kind == "latent" else HD ** -0.5
                        for a in schedule(kind):
                            g = a[1]
                            if a[0] == "proj" and kind != "latent":
                                high_part(q_part, L, ("pq", L, g), c("q_low"))
                                high_part(k_part, L, ("pk", L, g), c("k_low"))
                            elif a[0] == "proj":
                                for j in (2 * a[2], 2 * a[2] + 1):
                                    high_part(q_part, L, ("m2q", L, g, j), c("lq_low"), bq_m2_low[:])
                                    high_part(k_part, L, ("m2k", L, g, j), c("lk_low"))
                            elif a[0] == "st":
                                j = a[2]
                                n_group = NG * L + g
                                if j == 0 and n_group >= 2:
                                    act.wait_ge(o_full, n_group - 1)
                                for kt in range(QT):
                                    name = ("st", L, g, j, kt)
                                    lo = 0 if kind == "ffn" else kt * P
                                    act.wait_ge(st_full, SCORES[name] + 1)
                                    act.activation(probs[:, g % 2, j, kt, lo:T], st_bank(*name)[:, lo:T],
                                                   ACT.Exp, scale=scale).then_inc(st_free, 1)
                            elif a[0] == "av":
                                act.wait_ge(o_full, NG * L + g + 1)
                                if NG * L + g >= 2:
                                    prev = NG * L + g - 2
                                    act.wait_ge(misc_full, MISC["oT", prev // NG, prev % NG] + 1)
                                act.copy(os_[:, g % 2, :], ps[:, O_BANK, :]).then_inc(o_free, 1)
                        if kind != "ffn":
                            continue
                        f = FFN[L]
                        act.wait_ge(logits, f + 1)
                        act.activation(lg[:, 1], lg[:, 0], ACT.Exp).then_inc(exped, 1)
                        act.wait_ge(gdiff, f + 1)
                        act.activation(r4[:, 3], r4[:, 2], ACT.Exp).then_inc(exped, 1)
                        for e in range(E):
                            n = E * f + e
                            if n >= 2:
                                prev = n - 2
                                act.wait_ge(sm_full, SMAX["o", [L for L in FFN][prev // E], prev % E] + 1)
                            for ch in range(FC):
                                name = ("h", L, e, ch)
                                act.wait_ge(st_full, SCORES[name] + 1)
                                act.activation(hid[:, e % 2, ch, :], st_bank(*name), ACT.Gelu,
                                               bias=be1_sb[:, e * FC + ch:e * FC + ch + 1])\
                                    .then_inc(st_free, 1)

                @block.vector
                def _(dve):
                    n_step = 0
                    n_norm = 0
                    n_split = 0

                    def step(ins):
                        nonlocal n_step
                        n_step += 1
                        ins.then_inc(dve_step, 1)
                        dve.wait_ge(dve_step, n_step)

                    def tiles(col):
                        return col.unsqueeze(2).broadcast_to([P, QT, P])

                    def every_tile(row):
                        return row.unsqueeze(1).broadcast_to([P, QT, P])

                    def norm(dst, src, sem_out=None):
                        nonlocal n_norm
                        for t in range(QT):
                            ins = dve.bn_stats(st6[:, t, :], src[:, t, :])
                        step(ins)
                        for t in range(QT):
                            ins = dve.bn_aggr(mv[:, t, :], st6[:, t, :])
                        n_norm += 1
                        ins.then_inc(var_ready, 1)
                        dve.wait_ge(rstd_ready, n_norm)
                        for t in range(QT):
                            ins = dve.tensor_scalar(dst[:, t, :], src[:, t, :], mv[:, t, 0:1], rstd[:, t:t + 1],
                                                    ALU.subtract, ALU.mult)
                        if sem_out is None:
                            step(ins)
                        else:
                            ins.then_inc(sem_out, 1)

                    def misc(*name):
                        dve.wait_ge(misc_full, MISC[name] + 1)
                        return misc_bank(*name)

                    def freed(ins, name):
                        ins.then_inc(misc_free, 1)
                        dve.wait_ge(misc_free, MISC[name] + 1)

                    def tell(sem_out, n):
                        dve.nop().then_inc(sem_out, 1)

                    def split_into(dst, part, name, add):
                        nonlocal n_split
                        bank = misc(*name)
                        dve.wait_ge(parts, n_split + 1)
                        n_split += 1
                        ins = dve.scalar_tensor_tensor(out=dst, in0=bank, scalar=add, in1=part[:].bitcast(F32),
                                                       op0=ALU.add, op1=ALU.subtract)
                        freed(ins, name)
                        dve.nop().then_inc(split, 1)

                    dve.wait_ge(x_in, 16)
                    for L, kind in enumerate(LAYERS):
                        norm(ys, xs, y_ready)
                        freed(dve.tensor_copy(yT[:], misc("yT", L)), ("yT", L))
                        dve.nop().then_inc(yT_ready, 1)
                        if L > 0:
                            dve.wait_ge(o_full, NG * L)
                        freed(dve.tensor_copy(
                            va[:, :, :, 0:HD],
                            misc("v", L).rearrange("p (t h i) -> p t h i", t=QT, h=H)), ("v", L))
                        dve.nop().then_inc(v_ready, 1)

                        for a in schedule(kind):
                            g = a[1]
                            if a[0] == "proj":
                                if kind != "latent":
                                    split_into(qs[:, g % 2, g // 2, :], q_part, ("pq", L, g), c("zero"))
                                    split_into(ks[:, g % 2, g // 2, :], k_part, ("pk", L, g), c("k_one"))
                                    continue
                                pr = a[2]
                                if g >= 2:
                                    dve.wait_ge(st_full, SCORES["st", L, g - 2, 2 * pr + 1, QT - 1] + 1)
                                for m, n in enumerate(("m1q", "m1k")):
                                    bank = misc(n, L, g, pr)
                                    if 2 * g + pr > 0:
                                        pg, pj = (g, 1) if pr else (g - 1, 3)
                                        dve.wait_ge(misc_full, MISC["m2q" if m == 0 else "m2k", L, pg, pj] + 1)
                                    pair = 2 * g + pr
                                    ins = dve.scalar_tensor_tensor(
                                        out=r1[:, m, :], in0=bank, scalar=b_lat[:, m, pair:pair + 1],
                                        in1=c("cos_sin"), op0=ALU.add, op1=ALU.mult)
                                    freed(ins, (n, L, g, pr))
                                    dve.nop().then_inc(r1_ready, 1)
                                for j in (2 * pr, 2 * pr + 1):
                                    one = c("lk_one")[:, j:j + 1]
                                    split_into(qs[:, g % 2, j, :], q_part, ("m2q", L, g, j), bq_m2[:])
                                    split_into(ks[:, g % 2, j, :], k_part, ("m2k", L, g, j), one)
                            elif a[0] == "max":
                                j = a[2]
                                for qt in range(QT):
                                    name = ("s", L, g, j, qt)
                                    n = T if kind == "ffn" else (qt + 1) * P
                                    dve.wait_ge(sm_full, SMAX[name] + 1)
                                    dve.tensor_reduce(nmax[:, j, qt:qt + 1], sm_bank(*name)[:, 0:n], AX.X,
                                                      ALU.max, negate=True).then_inc(sm_free, 1)
                                if j < GH - 1:
                                    continue
                                dve.wait_ge(sm_free, SMAX["s", L, g, j, QT - 1] + 1)
                                if kind == "latent":
                                    cols = mx[:, 1, :, M_ROW_LAT:M_ROW_LAT + 2 * GH]\
                                        .rearrange("p t (j s) -> p j t s", s=2)
                                    high, low = cols[:, :, :, 0], cols[:, :, :, 1]
                                else:
                                    cols = mx[:, 0].rearrange("p t (j s) -> p j t s", s=32)
                                    high, low = cols[:, :, :, M_ROW], cols[:, :, :, M_ROW + 1]
                                if NG * L + g > 0:
                                    pl, pg = divmod(NG * L + g - 1, NG)
                                    dve.wait_ge(misc_full, MISC["mT", pl, pg] + 1)
                                step(dve.tensor_copy(high, nmax[:]))
                                dve.tensor_tensor(low, nmax[:], high.bitcast(F32), ALU.subtract)\
                                    .then_inc(maxima, 1)
                                dve.wait_ge(maxima, NG * L + g + 1)
                            elif a[0] == "maxT":
                                bank = misc("mT", L, g)
                                if kind == "latent":
                                    for j in range(GH):
                                        dst = qs[96:P, g % 2, j, :]
                                        ins = dve.tensor_copy(dst, bank[96:P, :])
                                else:
                                    dst = qs[:, g % 2, g // 2, :]
                                    ins = dve.tensor_tensor(dst, bank, dst.bitcast(F32), ALU.add)
                                freed(ins, ("mT", L, g))
                                dve.nop().then_inc(shifted, 1)
                            elif a[0] == "oT":
                                bank = misc("oT", L, g).rearrange("p (t j s) -> p t j s", t=QT, s=32)
                                step(dve.reciprocal(rden[:], bank[:, :, :, HD]))
                                dst = ctxs[:, :, g * 32:(g + 1) * 32].rearrange("p t (j i) -> p t j i", i=HD)
                                freed(dve.tensor_tensor(dst, bank[:, :, :, 0:HD],
                                                        rden[:].unsqueeze(3).broadcast_to([P, QT, GH, HD]),
                                                        ALU.mult), ("oT", L, g))
                        dve.nop().then_inc(ctx_ready, 1)
                        freed(dve.tensor_copy(ctxT[:], misc("cT", L)), ("cT", L))
                        dve.nop().then_inc(ctxT_ready, 1)
                        bank = misc("wo", L).rearrange("p (t d) -> p t d", t=QT)
                        if kind == "latent":
                            freed(dve.tensor_tensor(xs[:], bank, xs[:], ALU.add), ("wo", L))
                            step(dve.tensor_tensor(xs[:], xs[:], every_tile(bias_lat[:]), ALU.add))
                            continue
                        if kind == "causal":
                            freed(dve.tensor_tensor(xs[:], bank, xs[:], ALU.add), ("wo", L))
                            continue
                        f = FFN[L]
                        freed(dve.tensor_tensor(tmp[:], bank, ys[:], ALU.add), ("wo", L))
                        step(dve.tensor_tensor(tmp[:], tmp[:], every_tile(rows[:, 0, :]), ALU.add))
                        norm(zs, tmp)
                        step(dve.tensor_tensor(zs[:], zs[:], every_tile(rows[:, 1, :]), ALU.mult))
                        dve.tensor_tensor(zs[:], zs[:], every_tile(rows[:, 2, :]), ALU.add).then_inc(z_ready, 1)
                        freed(dve.tensor_copy(zT[:], misc("zT", L)), ("zT", L))
                        dve.nop().then_inc(zT_ready, 1)
                        bank = misc("rt", L)[:, 0:QT * E].rearrange("p (t e) -> p t e", t=QT)
                        step(dve.tensor_reduce(r4[:, 0], bank, AX.X, ALU.max))
                        over = [P, QT, E]
                        freed(dve.tensor_tensor(lg[:, 0], bank, r4[:, 0].unsqueeze(2).broadcast_to(over),
                                                ALU.subtract), ("rt", L))
                        dve.nop().then_inc(logits, 1)
                        dve.wait_ge(exped, 2 * f + 1)
                        step(dve.tensor_reduce(r4[:, 1], lg[:, 1], AX.X, ALU.add))
                        step(dve.reciprocal(r4[:, 1], r4[:, 1]))
                        step(dve.tensor_tensor(lg[:, 2], lg[:, 1], r4[:, 1].unsqueeze(2).broadcast_to(over),
                                               ALU.mult))
                        for t in range(QT):
                            step(dve.max(lg[:, 3, t, :], lg[:, 2, t, :]))
                            step(dve.max_index(lgi[:, t, :], lg[:, 3, t, :], lg[:, 2, t, :]))
                        step(dve.tensor_copy(lgf[:], lgi[:]))
                        dve.tensor_tensor(r4[:, 2], lg[:, 3, :, 1], lg[:, 3, :, 0], ALU.subtract)\
                            .then_inc(gdiff, 1)
                        dve.wait_ge(exped, 2 * f + 2)
                        step(dve.tensor_scalar(r4[:, 4], r4[:, 3], 1.0, None, ALU.add))
                        step(dve.reciprocal(r4[:, 4], r4[:, 4]))
                        step(dve.tensor_tensor(r4[:, 5], r4[:, 3], r4[:, 4], ALU.mult))
                        which = c("expert").unsqueeze(1).broadcast_to(over)
                        for n in range(2):
                            step(dve.tensor_tensor(lg[:, 3 + n], which,
                                                   lgf[:, :, n:n + 1].broadcast_to(over), ALU.is_equal))
                            step(dve.tensor_tensor(lg[:, 3 + n], lg[:, 3 + n],
                                                   r4[:, 4 + n].unsqueeze(2).broadcast_to(over), ALU.mult))
                        dve.tensor_tensor(lg[:, 5], lg[:, 3], lg[:, 4], ALU.add).then_inc(gates, 1)
                        dve.wait_ge(gates, f + 1)
                        for e in range(E):
                            if e == 1:
                                freed(dve.tensor_copy(gT[0:E, :], misc("gT", L)[0:E, :]), ("gT", L))
                                dve.nop().then_inc(gT_ready, 1)
                                bank = misc("be2", L).rearrange("p (t d) -> p t d", t=QT)
                                freed(dve.tensor_tensor(acc[:], bank, acc[:], ALU.add), ("be2", L))
                            name = ("o", L, e)
                            dve.wait_ge(sm_full, SMAX[name] + 1)
                            bank = sm_bank(*name).rearrange("p (t d) -> p t d", t=QT)
                            dst = acc if e == 0 else tmp
                            dve.tensor_tensor(dst[:], bank, tiles(lg[:, 5, :, e]), ALU.mult).then_inc(sm_free, 1)
                            dve.wait_ge(sm_free, SMAX[name] + 1)
                            if e > 0:
                                step(dve.tensor_tensor(acc[:], acc[:], tmp[:], ALU.add))
                        step(dve.tensor_tensor(acc[:], acc[:], zs[:], ALU.add))
                        norm(tmp, acc)
                        step(dve.tensor_tensor(tmp[:], tmp[:], every_tile(rows[:, 3, :]), ALU.mult))
                        step(dve.tensor_tensor(tmp[:], tmp[:], every_tile(rows[:, 4, :]), ALU.add))
                        ins = dve.tensor_tensor(xs[:], xs[:], tmp[:], ALU.add)
                        if L == len(LAYERS) - 1:
                            ins.then_inc(seq_done, 1)
                        else:
                            step(ins)

            nc.all_engine_barrier()
            for s in turn_sems:
                nc.gpsimd.sem_clear(s)
            nc.all_engine_barrier()


PREP_REP = 5 + 5 + 3 + 6
PREP_BLOCKD = PREP_REP + 2 + 6 + 2 + 1
PREP_OUT = PREP_BLOCKD - 1 + 6 + 3 + 3

_INS = ["L0_attn_a_x", "L0_attn_a_c_attn_w", "L0_attn_a_c_attn_b", "L0_attn_a_q2l_w", "L0_attn_a_q2l_b",
        "L0_attn_a_kv2l_w", "L0_attn_a_kv2l_b", "L0_attn_a_l2o_w", "L0_attn_a_l2o_b", "L0_attn_a_wqk_w",
        "L0_attn_a_wqk_b", "L0_attn_a_cproj_w", "L0_attn_a_cproj_b", "L0_attn_b_w_qkv", "L0_attn_b_w_o",
        "L0_ffn_Wq", "L0_ffn_Wk", "L0_ffn_Wv", "L0_ffn_Wo", "L0_ffn_bo", "L0_ffn_Wr", "L0_ffn_We1",
        "L0_ffn_be1", "L0_ffn_We2", "L0_ffn_be2", "L0_ffn_ln1_g", "L0_ffn_ln1_b", "L0_ffn_ln2_g",
        "L0_ffn_ln2_b"]


def kernel(**inputs):
    import concourse.bacc as bacc
    from concourse.bass_utils import run_bass_kernel_spmd

    nc = bacc.Bacc("TRN2", target_bir_lowering=False, num_devices=1)
    arrays, args = {}, []
    for name in _INS:
        a = np.ascontiguousarray(inputs[name])
        arrays[name + "_dram"] = a
        args.append(nc.dram_tensor(name + "_dram", a.shape, mybir.dt.from_np(a.dtype), kind="ExternalInput").ap())
    arrays["const_dram"] = CONST
    args.append(nc.dram_tensor("const_dram", CONST.shape, F32, kind="ExternalInput").ap())
    args.append(nc.dram_tensor("out_dram", (4, T, P), F32, kind="ExternalOutput").ap())
    hybrid_kernel(nc, *args)
    r = run_bass_kernel_spmd(nc, [arrays], core_ids=[0])
    return r.results[0]["out_dram"]
```

```python
from contextlib import ExitStack

import numpy as np

import concourse.bass as bass
from concourse import mybir
from concourse.alu_op_type import AluOpType as ALU

ACT = mybir.ActivationFunctionType
AX = mybir.AxisListType
F32 = mybir.dt.float32
F32R = mybir.dt.float32r
BF16 = mybir.dt.bfloat16
U32 = mybir.dt.uint32

P = 128
T = 512
QT = T // P
H = 16
HD = 8
LAT = 32
GH = 4
NG = H // GH
E = 8
FC = 4
NEG = -1e30
LAYERS = ("latent", "ffn", "causal", "ffn")
M_ROW = 24
LEAD, GRAIN, SWITCH = 20000, 100, 500
SOON = {}
M_ROW_LAT = 96


def constants():
    cols, at, n = [], {}, 0

    def put(name, a):
        nonlocal n
        full = np.zeros((P, a.shape[1]), np.float32)
        full[: a.shape[0]] = a
        cols.append(full)
        at[name] = (n, n + a.shape[1])
        n += a.shape[1]

    eye = np.eye(P, dtype=np.float32)
    i = np.arange(P)
    put("ident", eye)
    put("mask_qk", np.where(i[None, :] > i[:, None], np.float32(NEG), np.float32(0)))
    put("mask_kq", np.where(i[:, None] > i[None, :], np.float32(NEG), np.float32(0)))
    exponent = np.arange(0, LAT, 2, dtype=np.float32) / np.float32(LAT)
    inv = (np.float32(1.0) / np.power(np.float32(10000.0), exponent)).astype(np.float32)
    freqs = np.outer(np.arange(T, dtype=np.float32), inv).astype(np.float32)
    cos = np.repeat(np.cos(freqs), 2, axis=1).T.astype(np.float32)
    sin = np.repeat(np.sin(freqs), 2, axis=1).T.astype(np.float32)
    put("cos_sin", np.concatenate([cos, sin, cos, sin]))
    put("own_head", (i[:, None] // HD == np.arange(H)[None, :]).astype(np.float32))
    i32 = np.eye(LAT, dtype=np.float32)
    rot_t = np.zeros((LAT, LAT), np.float32)
    for k in range(0, LAT, 2):
        rot_t[k + 1, k] = -1.0
        rot_t[k, k + 1] = 1.0
    put("sum3", np.tile(np.concatenate([i32, i32, i32, np.zeros_like(i32)], 1), (4, 1)))
    s = i % 32
    put("q_low", ((s >= 8) & (s < 16)).astype(np.float32)[:, None])
    put("k_low", ((s >= 16) & (s < 24)).astype(np.float32)[:, None])
    put("k_one", ((s == M_ROW) | (s == M_ROW + 1)).astype(np.float32)[:, None])
    put("lq_low", ((i >= 32) & (i < 64)).astype(np.float32)[:, None])
    put("lk_low", ((i >= 64) & (i < 96)).astype(np.float32)[:, None])
    put("lk_one", np.stack([(i - M_ROW_LAT) // 2 == j for j in range(GH)], 1).astype(np.float32))
    put("zero", np.zeros((P, 1), np.float32))
    put("expert", np.tile(np.arange(E, dtype=np.float32)[None], (P, 1)))
    put("neg_half", np.full((P, QT), -0.5, np.float32))
    put("eye_rot", np.concatenate([i32, rot_t], 1))
    put("eye_rot2", np.concatenate([i32, rot_t, i32, rot_t], 1))
    put("eye4", np.tile(i32, (1, 4)))
    return np.concatenate(cols, 1), at


CONST, CONST_AT = constants()


PASS, TURN, ROWS = 216, 430, 880
LATENCY = {"pe": 200, "dve": 180, "act": 220, "pool": 160}
TABLE = 1300


def sequence_tasks(s):
    t = {}

    def add(eng, name, ns, *before):
        t[eng, name] = (ns, [b for b in before if b is not None])

    for L, kind in enumerate(LAYERS):
        def span(n):
            return PASS * n // QT + (60 if kind != "ffn" else 0)

        here = (s, L)
        last = [("dve", ("end", s, L - 1))] if L else []
        add("dve", ("norm", *here), 1240, *last)
        add("pool", ("norm", *here), 1300, ("dve", ("norm", *here)))
        add("dve", ("apply", *here), 1030, ("pool", ("norm", *here)))
        add("pe", ("yT", *here), TURN, ("dve", ("apply", *here)))
        add("dve", ("yT", *here), 600, ("pe", ("yT", *here)))
        add("pe", ("v", *here), ROWS, ("dve", ("yT", *here)))
        add("dve", ("v", *here), 600, ("pe", ("v", *here)))
        for g in range(NG):
            used = ("pe", ("st", s, L, g - 2, 0, GH - 1)) if g >= 2 else None
            if kind != "latent":
                for n, ns in (("pq", 663), ("pk", 4 * 663)):
                    name = (n, s, L, g)
                    add("pe", name, 4 * PASS, ("dve", ("yT", *here)), ("pe", ("pk", s, L, g - 1)) if g else None)
                    add("act", name, 575, ("pe", name))
                    add("dve", name, ns, ("act", name), used)
            else:
                for j in range(GH):
                    for m in "qk":
                        one, two = ("m1" + m, s, L, g, j // 2), ("m2" + m, s, L, g, j)
                        if j % 2 == 0:
                            p = 2 * g + j // 2 - 1
                            prev = ("pe", ("m2" + m, s, L, p // 2, 2 * (p % 2) + 1)) if p >= 0 else None
                            add("pe", one, 4 * PASS, ("dve", ("yT", *here)), prev)
                            add("dve", one, 663, ("pe", one), prev)
                        before = ("pe", ("m2" + m, s, L, g, j - 1)) if j % 2 else None
                        add("pe", two, 4 * PASS, ("dve", one), before)
                        add("act", two, 620, ("pe", two))
                        add("dve", two, 663, ("act", two), used)
            for j in range(GH):
                for qt in range(QT):
                    n = QT if kind == "ffn" else qt + 1
                    name = ("max", s, L, g, j, qt)
                    made = [("m2q", s, L, g, j), ("m2k", s, L, g, j)] if kind == "latent" else \
                        [("pq", s, L, g), ("pk", s, L, g)]
                    k = QT * j + qt - 1
                    order = ("pe", ("max", s, L, g, k // QT, k % QT)) if k >= 0 else None
                    add("pe", name, span(n), *(("dve", x) for x in made), order)
                    add("dve", name, 65 + 133 * n, ("pe", name), ("dve", ("fold", s, L, g - 1)) if g else None,
                        ("dve", order[1]) if order else None)
            fold, up = ("fold", s, L, g), ("mT", s, L, g)
            add("dve", fold, 300, ("dve", ("max", s, L, g, GH - 1, QT - 1)), ("pe", ("mT", s, L, g - 1)) if g else None)
            add("pe", up, TURN, ("dve", fold))
            add("dve", up, 600, ("pe", up), ("act", ("mT", s, L, g - 1)) if g and kind == "latent" else None)
            if kind == "latent":
                add("act", up, 1900, ("dve", up))
            shifted = ("act" if kind == "latent" else "dve", up)
            order = ("pe", ("st", s, L, g - 1, 0, GH - 1)) if g else None
            for kt in reversed(range(QT)):
                w = QT if kind == "ffn" else QT - kt
                for j in range(GH):
                    name = ("st", s, L, g, kt, j)
                    add("pe", name, span(w), shifted, order)
                    add("act", name, 50 + 107 * w, ("pe", name), ("act", order[1]) if order else None)
                    order = ("pe", name)
                name = ("av", s, L, g, kt)
                prev = ("pe", ("av", s, L, g, kt + 1)) if kt < QT - 1 else \
                    ("act", ("av", s, L, g - 1, 0)) if g else None
                add("pe", name, 4 * PASS * w // QT + 60, ("dve", ("v", *here)), ("act", ("st", s, L, g, kt, GH - 1)), prev)
            add("act", ("av", s, L, g, 0), 480, ("pe", ("av", s, L, g, 0)), ("pe", ("oT", s, L, g - 1)) if g else None)
            add("pe", ("oT", s, L, g), TURN, ("act", ("av", s, L, g, 0)))
            add("dve", ("oT", s, L, g), 500, ("pe", ("oT", s, L, g)))
        add("pe", ("cT", *here), TURN, *(("dve", ("oT", s, L, g)) for g in range(NG)))
        add("dve", ("cT", *here), 600, ("pe", ("cT", *here)))
        add("pe", ("wo", *here), ROWS, ("dve", ("cT", *here)))
        if kind != "ffn":
            add("dve", ("wo", *here), 1400 if kind == "latent" else 700, ("pe", ("wo", *here)))
            if kind == "latent" and s == 1:
                add("pool", ("zero", *here), 3500, ("pe", ("cT", *here)))
            add("dve", ("end", *here), 0, ("dve", ("wo", *here)))
            continue
        add("dve", ("wo", *here), 2700, ("pe", ("wo", *here)))
        add("pool", ("wo", *here), 1300, ("dve", ("wo", *here)))
        add("dve", ("z", *here), 2500, ("pool", ("wo", *here)))
        add("pe", ("zT", *here), TURN, ("dve", ("z", *here)))
        add("dve", ("zT", *here), 600, ("pe", ("zT", *here)))
        add("pe", ("rt", *here), 430, ("dve", ("zT", *here)))
        add("dve", ("rt", *here), 400, ("pe", ("rt", *here)))
        add("act", ("rt", *here), 150, ("dve", ("rt", *here)))
        add("dve", ("top", *here), 1800, ("act", ("rt", *here)))
        add("act", ("top", *here), 120, ("dve", ("top", *here)))
        add("dve", ("gate", *here), 1600, ("act", ("top", *here)))
        add("pe", ("gT", *here), TURN, ("dve", ("gate", *here)))
        add("dve", ("gT", *here), 600, ("pe", ("gT", *here)))
        add("pe", ("be2", *here), ROWS, ("dve", ("gT", *here)))
        for e in range(E):
            for ch in range(FC):
                h = ("h", s, L, e, ch)
                k = FC * e + ch - 1
                add("pe", h, 4 * PASS, ("dve", ("zT", *here)), ("pe", ("h", s, L, k // FC, k % FC)) if k >= 0 else None)
                add("act", h, 575, ("pe", h), ("act", ("h", s, L, k // FC, k % FC)) if k >= 0 else None)
            o = ("o", s, L, e)
            add("pe", o, 16 * PASS, ("act", h), ("pe", ("o", s, L, e - 1)) if e else None)
            add("dve", o, 1350 if e else 650, ("pe", o), ("dve", ("gate", *here)))
        add("dve", ("be2", *here), 2700, ("pe", ("be2", *here)), ("dve", o))
        add("pool", ("be2", *here), 1300, ("dve", ("be2", *here)))
        add("dve", ("end", *here), 3250, ("pool", ("be2", *here)))
    return t


class Plan:

    RINGS = {"misc": ("yT", "v", "pq", "pk", "m1q", "m1k", "m2q", "m2k", "mT", "oT", "cT", "wo", "zT",
                      "rt", "gT", "be2"),
             "scores": ("st", "h"), "smax": ("max", "o")}
    COUNTED = {"values": ("pe", ("av",)), "copies": ("act", ("av",)), "parts": ("act", ("pq", "pk", "m2q", "m2k")),
               "stats": ("dve", ("norm", "wo", "be2")), "applied": ("dve", ("apply",)),
               "folds": ("dve", ("fold",)), "shifts": ("act", ("mT",)), "zs": ("dve", ("z",)),
               "routes": ("dve", ("rt",)), "tops": ("dve", ("top",)), "gates": ("dve", ("gate",)),
               "exps": ("act", ("rt", "top"))}
    BANKS = 6
    SLOTS = 4

    def __init__(self, lead=LEAD, grain=GRAIN, switch=SWITCH, soon=SOON):
        tasks = {}
        for s in range(2):
            tasks.update(sequence_tasks(s))
        ns, before = tasks["dve", ("norm", 1, 0)]
        tasks["dve", ("norm", 1, 0)] = (ns, before + [("dve", ("oT", 0, 0, NG - 1))])
        ns, before = tasks["dve", ("pk", 1, 1, 0)]
        tasks["dve", ("pk", 1, 1, 0)] = (ns, before + [("pool", ("zero", 1, 0))])
        reader = {"misc": "dve", "scores": "act", "smax": "dve"}
        for (eng, name), (ns, before) in list(tasks.items()):
            ring = next((r for r, members in self.RINGS.items() if name[0] in members), None)
            if eng == "pe" and ring:
                more = [x for x in tasks[reader[ring], name][1] if x[1][0] != name[0]]
                tasks[eng, name] = (ns, before + more)
        after = {k: [] for k in tasks}
        for k, (_, before) in tasks.items():
            for x in before:
                after[x].append(k)
        rank, open_ = {}, {k: len(v) for k, v in after.items()}
        stack = [k for k, n in open_.items() if n == 0]
        while stack:
            k = stack.pop()
            rank[k] = tasks[k][0] + max((rank[a] + LATENCY[k[0]] for a in after[k]), default=0)
            for x in tasks[k][1]:
                open_[x] -= 1
                if open_[x] == 0:
                    stack.append(x)
        self.order = {"pe": [], "dve": [], "act": [], "pool": []}
        self.n = {r: {} for r in (*self.RINGS, *self.COUNTED)}
        self.n_read = {r: {} for r in self.RINGS}
        self.slot, self.before, self.bank, self.bank_before = {}, {}, {}, {}
        end, clock = {}, dict.fromkeys(self.order, 0)
        banks, filled = [(0, n) for n in range(self.BANKS)], {}
        table = "exp"
        free, owner = [(0, n) for n in range(self.SLOTS)], {}
        missing = {k: len(v[1]) for k, v in tasks.items()}
        ready = [k for k, n in missing.items() if n == 0]
        while ready:
            best = None
            for k in ready:
                eng, name = k
                what = name[0]
                start = max([clock[eng]] + [end[x] + LATENCY[x[0]] for x in tasks[k][1]])
                ring = next((r for r, members in self.RINGS.items() if what in members), None)
                if ring and eng == "pe":
                    if not banks:
                        continue
                    start = max(start, min(banks)[0])
                if eng == "act" and what in ("pq", "pk", "m2q", "m2k"):
                    before = list(self.n["parts"])[-2:]
                    if len(before) == 2:
                        if ("dve", before[0]) not in end:
                            continue
                        start = max(start, end["dve", before[0]] + LATENCY["dve"])
                done = sum(x[0] in ("norm", "wo", "be2") for x in self.order["pool"])
                if eng == "pool" and what in ("norm", "wo", "be2") and \
                        list(self.n["stats"])[done:done + 1] != [name]:
                    continue
                if eng == "pe" and what in ("st", "h") and name[-1] == 0:
                    if not free:
                        continue
                    start = max(start, min(free)[0])
                if what in ("st", "rt", "top", "h") and eng == "act" and (what == "h") != (table == "gelu"):
                    start += TABLE
                wait = start
                if ring == "scores" and eng == "pe" and self.n[ring] and next(reversed(self.n[ring]))[0] != what:
                    wait += switch
                key = (wait // grain, -rank[k] - (lead if name[1] == 0 else 0) - soon.get(what, 0))
                if best is None or key < best[0]:
                    best = (key, k, start, ring)
            assert best, "the tasks wait for each other"
            _, k, start, ring = best
            eng, name = k
            what = name[0]
            ready.remove(k)
            end[k] = clock[eng] = start + tasks[k][0]
            self.order[eng].append(name)
            if what in ("st", "rt", "top", "h") and eng == "act":
                table = "gelu" if what == "h" else "exp"
            if ring and eng == "pe":
                self.add(ring, name)
                banks.sort()
                self.bank[name] = banks.pop(0)[1]
                self.bank_before[name] = filled.get(self.bank[name])
                filled[self.bank[name]] = (ring, name)
            if ring and eng == reader[ring]:
                self.n_read[ring][name] = len(self.n_read[ring])
                banks.append((end[k] + LATENCY[eng], self.bank[name]))
            for count, (who, members) in self.COUNTED.items():
                if eng == who and what in members:
                    if count == "copies" and name[4] or count == "stats" and what != "norm" and \
                            LAYERS[name[2]] != "ffn":
                        continue
                    self.add(count, name)
            if eng == "pe" and what in ("st", "h") and name[-1] == 0:
                unit = ("av" if what == "st" else "o", *name[1:-1])
                free.sort()
                self.slot[unit] = free.pop(0)[1]
                self.before[unit] = owner.get(self.slot[unit])
                owner[self.slot[unit]] = unit
            if eng == "pe" and what in ("av", "o"):
                free.append((end[k] + LATENCY["pe"], self.slot[name]))
            for a in after[k]:
                missing[a] -= 1
                if missing[a] == 0:
                    ready.append(a)
        assert len(end) == len(tasks)
        self.length = max(end.values())

    def add(self, ring, name):
        self.n[ring][name] = len(self.n[ring])

    def count(self, ring, *name):
        return self.n[ring][name] + 1

    def read(self, ring, *name):
        return self.n_read[ring][name] + 1


PLAN = Plan()


def hybrid_kernel(nc, x, wa, ba, q2l, q2lb, kv2l, kv2lb, l2o, l2ob, wqk, wqkb, cproj, cprojb,
                  wqkv, wo_b, wq, wk, wv, wo, bo, wr, we1, be1, we2, be2, g1, b1, g2, b2, const, out):
    with ExitStack() as ctx:
        def sb(name, shape, dt=F32):
            return ctx.enter_context(nc.sbuf_tensor(name, shape, dt))

        def sem(name):
            return ctx.enter_context(nc.semaphore(name))

        ps = ctx.enter_context(nc.psum_tensor("ps", [P, 8, T], F32))
        O_BANK = (Plan.BANKS, Plan.BANKS + 1)

        cst = sb("cst", [P, CONST.shape[1]])
        ident_bf = sb("ident_bf", [P, P], BF16)
        mask_bf = sb("mask_bf", [P, 2, P], BF16)
        small = sb("small", [P, 128])
        wrep = sb("wrep", [P, 4, NG, P])
        w_v = sb("w_v", [P, 3, P])
        w_o = sb("w_o", [P, 3, P])
        w_lat = sb("w_lat", [P, 2, H, 2 * LAT])
        b_lat = sb("b_lat", [P, 2, H // 2])
        w_m2q = sb("w_m2q", [P, P])
        bq_m2 = sb("bq_m2", [P, 1])
        bq_m2_low = sb("bq_m2_low", [P, 1])
        cvec = sb("cvec", [P, 1])
        bias_lat = sb("bias_lat", [P, P])
        rows = sb("rows", [P, 6, P])
        wr_sb = sb("wr_sb", [P, E])
        we1_sb = sb("we1_sb", [P, E, FC * P])
        we2_sb = sb("we2_sb", [P, E, FC, P])
        be1_sb = sb("be1_sb", [P, E * FC])
        be2_sb = sb("be2_sb", [P, P])
        xs = sb("xs", [P, 2, QT, P])
        ys = sb("ys", [P, 2, QT, P])
        turned = sb("turned", [P, 2, T])
        va = sb("va", [P, 2, QT, H, 2 * HD])
        os_ = sb("os_", [P, 2, T])
        ctxs = sb("ctxs", [P, 2, QT, P])
        zs = sb("zs", [P, 2, QT, P])
        gates = sb("gates", [P, 2, QT, E])
        q_x = sb("q_x", [P, 2, T], F32R)
        k_ops = sb("k_ops", [P, 2, 2, GH, T], F32R)
        nmax = sb("nmax", [P, 2, GH, QT])
        mx = sb("mx", [P, 2, QT, P], F32R)
        mx_lat = sb("mx_lat", [P, QT, P], F32R)
        q_lat = sb("q_lat", [P, 2, GH, T], F32R)
        m_rows = sb("m_rows", [P, T])
        part = sb("part", [P, 2, T], F32R)
        r1 = sb("r1", [P, 2, T])
        wide = sb("wide", [P, Plan.SLOTS, GH, T])
        tmp = sb("tmp", [P, QT, P])
        cprojT, bcast = zs[:, 0, 0, :], zs[:, 0, 1:3, :]
        rden = sb("rden", [P, QT, GH])
        st6 = sb("st6", [P, QT, 6])
        vare = sb("vare", [P, QT])
        mv = sb("mv", [P, 2, QT, 2])
        rstd = sb("rstd", [P, 2, QT])
        lg = sb("lg", [P, 2, 5, QT, E])
        lgi = sb("lgi", [P, 2, QT, E], U32)
        lgf = sb("lgf", [P, QT, E])
        r4 = sb("r4", [P, 2, 6, QT])

        raw = wide[:].rearrange("p e c n -> p (e c n)")[:, 0:9 * P].rearrange("p (m n) -> p m n", n=P)
        blockd = r1[:].rearrange("p m (h l) -> p (m h) l", l=2 * LAT)

        def c(name):
            a, b = CONST_AT[name]
            return cst[:, a:b]

        loaded = sem("loaded")
        prep_pe = sem("prep_pe")
        prep_dve = sem("prep_dve")

        with nc.Block() as block:
            n_loads = [0]

            @block.sync
            def _(sp):
                def load(dst, src):
                    n_loads[0] += 1
                    sp.dma_start(dst, src, allow_slow_non_contiguous=True).then_inc(loaded, 16)

                def every_partition(a, n, p=P):
                    return a.rearrange("(o n) -> o n", o=1).broadcast_to([p, n])

                load(cst[:], const)
                load(raw[:, 0:3, :], wa.rearrange("(s o) d -> o s d", s=3))
                load(raw[:, 3, :], cproj)
                load(raw[:, 4:7, :], wqkv.rearrange("s h k m -> (h k) s m"))
                load(raw[:, 7, :], wo_b)
                load(small[:, 0:3], ba.rearrange("(s o) -> o s", s=3))
                load(small[0:LAT, 4:12], q2l)
                load(small[0:LAT, 12:20], kv2l)
                load(small[0:LAT, 20:21], q2lb.rearrange("(n o) -> n o", o=1))
                load(small[0:LAT, 21:22], kv2lb.rearrange("(n o) -> n o", o=1))
                load(small[0:LAT, 24:32], l2o.rearrange("o l -> l o"))
                load(small[0:LAT, 32:64], wqk.rearrange("o l -> l o"))
                for r in range(3):
                    load(small[r * LAT:(r + 1) * LAT, 64:65], wqkb.rearrange("(n o) -> n o", o=1))
                for h in range(H):
                    load(small[h * HD:(h + 1) * HD, 65:66], l2ob.rearrange("(n o) -> n o", o=1))
                load(raw[:, 8, :], wq)
                load(bcast[:, 0, :], wk)
                load(w_v[:, 1, :], wv)
                load(w_o[:, 1, :], wo)
                for r, a in enumerate((bo, g1, b1, g2, b2, cprojb)):
                    load(rows[:, r, :], every_partition(a, P))
                load(wr_sb[:], wr)
                load(be1_sb[:], be1.rearrange("e (c p) -> p (e c)", p=P))
                load(be2_sb[0:E, :], be2)
                load(be2_sb[32:32 + E, :], be2)
                load(we1_sb[:], we1.rearrange("e d f -> d e f"))
                load(we2_sb[:], we2.rearrange("e (c p) d -> p e c d", p=P))

            @block.vector
            def _(dve):
                done = [0]

                def step(ins):
                    done[0] += 1
                    ins.then_inc(prep_dve, 1)
                    dve.wait_ge(prep_dve, done[0])

                step(dve.memset(va[:], 1.0))
                step(dve.memset(ps[:, O_BANK[0]:O_BANK[1] + 1, :], 0.0))
                step(dve.memset(w_m2q[:], 0.0))
                step(dve.memset(wrep[:], 0.0))
                step(dve.memset(bq_m2[:], 0.0))
                step(dve.memset(mx[:].bitcast(F32), 0.0))
                step(dve.memset(mx_lat[:].bitcast(F32), 0.0))
                step(dve.memset(k_ops[:, 0].bitcast(F32), 0.0))
                dve.wait_ge(loaded, 16 * n_loads[0])
                step(dve.tensor_copy(ident_bf[:], c("ident")))
                step(dve.tensor_copy(mask_bf[:, 0, :], c("mask_qk")))
                step(dve.tensor_copy(mask_bf[:, 1, :], c("mask_kq")))
                step(dve.tensor_copy(bq_m2[0:96, :], small[0:96, 64:65]))
                step(dve.tensor_tensor(bq_m2_low[:], bq_m2[:], c("lq_low"), ALU.mult))
                for n, col in enumerate((4, 12, 24)):
                    step(dve.tensor_copy(tmp[0:LAT, n, :].rearrange("p (h i) -> p h i", h=H),
                                         small[0:LAT, col:col + HD].unsqueeze(1).broadcast_to([LAT, H, HD])))
                for m, src in enumerate((raw[:, 8, :], bcast[:, 0, :])):
                    for r in range(3):
                        step(dve.tensor_copy(
                            wrep[:, m].rearrange("p g (j s) -> p (g j) s", j=GH)[:, :, 8 * r:8 * r + 8],
                            src.rearrange("p (h i) -> p h i", h=H)))
                ready = done[0]
                assert ready == PREP_REP
                dve.wait_ge(prep_pe, 1)
                step(dve.tensor_copy(w_v[:, 0, :], ps[:, 0, 0:P]))
                step(dve.tensor_copy(cprojT[:], ps[:, 0, P:2 * P]))
                for m in range(2):
                    for r in range(3):
                        step(dve.tensor_copy(
                            wrep[:, 2 + m].rearrange("p g (j s) -> p (g j) s", j=GH)[:, :, 8 * r:8 * r + 8],
                            ps[:, 0, (2 + m) * P:(3 + m) * P].rearrange("p (h i) -> p h i", h=H)))
                step(dve.tensor_copy(w_v[:, 2, :], ps[:, 1, 0:P]))
                step(dve.tensor_copy(w_o[:, 2, :], ps[:, 1, P:2 * P]))
                for m in range(2):
                    dve.wait_ge(prep_pe, 2 + 2 * m)
                    step(dve.tensor_tensor(
                        blockd, ps[:, 2, 64 * m:64 * m + 64].unsqueeze(1).broadcast_to([P, H, 64]),
                        c("own_head").unsqueeze(2).broadcast_to([P, H, 64]), ALU.mult))
                    dve.wait_ge(prep_pe, 3 + 2 * m)
                    step(dve.tensor_copy(w_lat[:, m].rearrange("p h l -> p (h l)"),
                                         ps[:, 3:5, :].rearrange("p a b -> p (a b)")))
                    step(dve.tensor_copy(b_lat[:, m, :], ps[:, 5, 0:H // 2]))
                for r in range(3):
                    step(dve.tensor_copy(w_m2q[:, r * LAT:(r + 1) * LAT], ps[:, 2, 128:160]))
                step(dve.tensor_tensor(
                    bcast[:, 0, :].rearrange("p (h i) -> p h i", h=H),
                    ps[:, 2, 160:168].unsqueeze(1).broadcast_to([P, H, HD]),
                    c("own_head").unsqueeze(2).broadcast_to([P, H, HD]), ALU.mult))
                step(dve.tensor_tensor(cvec[:], ps[:, 2, 168:169], small[:, 65:66], ALU.add))
                step(dve.tensor_copy(bcast[:, 1, :], cvec[:, 0:1].broadcast_to([P, P])))
                dve.wait_ge(prep_pe, 6)
                step(dve.tensor_copy(w_o[:, 0, :], ps[:, 0, 0:P]))
                step(dve.tensor_copy(tmp[:, 3, :], small[:, 2:3].broadcast_to([P, P])))
                dve.wait_ge(prep_pe, 7)
                step(dve.tensor_tensor(bias_lat[:], ps[:, 1, 0:P], rows[:, 5, :], ALU.add))

            @block.tensor
            def _(pe):
                ident = c("ident")
                pe.wait_ge(loaded, 16 * n_loads[0])
                pe.transpose(ps[:, 0, 0:P], raw[:, 2, :], ident)
                pe.transpose(ps[:, 0, P:2 * P], raw[:, 3, :], ident)
                pe.transpose(ps[:, 0, 2 * P:3 * P], raw[:, 4, :], ident)
                pe.transpose(ps[:, 0, 3 * P:4 * P], raw[:, 5, :], ident)
                pe.transpose(ps[:, 1, 0:P], raw[:, 6, :], ident)
                pe.transpose(ps[:, 1, P:2 * P], raw[:, 7, :], ident).then_inc(prep_pe, 1)
                pe.wait_ge(prep_dve, PREP_REP)
                pe.matmul(ps[:, 2, 0:64], tmp[0:LAT, 0, :], c("eye_rot")[0:LAT], start=True, stop=True,
                          skip_group_check=True)
                pe.matmul(ps[:, 2, 64:128], tmp[0:LAT, 1, :], c("eye_rot")[0:LAT], start=True, stop=True,
                          skip_group_check=True)
                pe.matmul(ps[:, 2, 128:160], c("eye4")[0:LAT], small[0:LAT, 32:64], start=True, stop=True,
                          skip_group_check=True)
                pe.matmul(ps[:, 2, 160:168], tmp[0:LAT, 2, :], small[0:LAT, 12:20], start=True, stop=True,
                          skip_group_check=True)
                pe.matmul(ps[:, 2, 168:169], tmp[0:LAT, 2, :], small[0:LAT, 21:22], start=True, stop=True,
                          skip_group_check=True).then_inc(prep_pe, 1)
                for m in range(2):
                    pe.wait_ge(prep_dve, PREP_BLOCKD + 3 * m)
                    bd = blockd.rearrange("p h l -> p (h l)")
                    for half in range(2):
                        pe.matmul(ps[:, 3 + half, :], raw[:, m, :], bd[:, half * T:(half + 1) * T],
                                  start=True, stop=True)
                    for pair in range(H // 2):
                        pe.matmul(ps[:, 5, pair:pair + 1], bd[:, pair * P:(pair + 1) * P], small[:, m:m + 1],
                                  start=True, stop=False, skip_group_check=True)
                        ins = pe.matmul(ps[:, 5, pair:pair + 1], c("eye_rot2")[0:LAT],
                                        small[0:LAT, 20 + m:21 + m], start=False, stop=True,
                                        skip_group_check=True)
                    ins.then_inc(prep_pe, 1)
                    if m == 0:
                        pe.matmul(ps[:, 2, 192:256], tmp[0:LAT, 1, :], c("eye_rot")[0:LAT], start=True,
                                  stop=True).then_inc(prep_pe, 1)
                pe.wait_ge(prep_dve, PREP_OUT)
                pe.matmul(ps[:, 0, 0:P], bcast[:, 0, :], cprojT[:], start=True, stop=True).then_inc(prep_pe, 1)
                pe.wait_ge(prep_dve, PREP_OUT + 2)
                pe.matmul(ps[:, 1, 0:P], bcast[:, 1, :], cprojT[:], start=True, stop=False)
                pe.matmul(ps[:, 1, 0:P], tmp[:, 3, :], w_o[:, 0, :], start=False, stop=True).then_inc(prep_pe, 1)

        x_in = sem("x_in")
        misc_full = sem("misc_full")
        misc_done = sem("misc_done")
        st_full = sem("st_full")
        st_done = sem("st_done")
        sm_full = sem("sm_full")
        sm_done = sem("sm_done")
        av_done = sem("av_done")
        o_copied = sem("o_copied")
        parts = sem("parts")
        normed = sem("normed")
        folded = sem("folded")
        shifted = sem("shifted")
        z_ready = sem("z_ready")
        logits = sem("logits")
        exped = sem("exped")
        gdiff = sem("gdiff")
        gated = sem("gated")
        var_ready = sem("var_ready")
        rstd_ready = sem("rstd_ready")
        dve_step = sem("dve_step")
        pool_step = sem("pool_step")
        zeroed = sem("zeroed")
        seq_done = sem("seq_done")
        stored = sem("stored")
        turn_sems = [x_in, misc_full, misc_done, st_full, st_done, sm_full, sm_done, av_done, o_copied,
                     parts, normed, folded, shifted, z_ready, logits, exped, gdiff, gated, var_ready,
                     rstd_ready, dve_step, pool_step, zeroed, seq_done, stored]

        xv = x.rearrange("(n s) (t p) d -> n s p t d", p=P, s=2)
        ov = out.rearrange("(n s) (t p) d -> n s p t d", p=P, s=2)
        LAST = len(LAYERS) - 1
        count, read = PLAN.count, PLAN.read

        def bank_of(*name):
            return ps[:, PLAN.bank[name], :]

        def queries(s, L, g, j):
            if LAYERS[L] == "latent":
                return q_lat[:, g % 2, j, :]
            return q_x[:, g % 2, :] if s == 0 else q_lat[:, g % 2, 0, :]

        def keys(s, L, g, j):
            return k_ops[:, 1 if LAYERS[L] == "latent" else s, g % 2, j, :]

        with nc.Fori(0, x.shape[0] // 2) as b:
            with nc.Block() as block:

                @block.sync
                def _(sp):
                    for s in range(2):
                        sp.dma_start(xs[:, s], xv[b, s]).then_inc(x_in, 16)
                    ends = [n for n in PLAN.order["dve"] if n[0] == "end" and n[2] == LAST]
                    for k, name in enumerate(ends):
                        sp.wait_ge(seq_done, k + 1)
                        sp.dma_start(ov[b, name[1]], xs[:, name[1]]).then_inc(stored, 16)
                    sp.wait_ge(stored, 32)

                @block.gpsimd
                def _(pool):
                    for name in PLAN.order["pool"]:
                        what, s, L = name[:3]
                        if name in PLAN.n["stats"]:
                            n = count("stats", *name)
                            eps = 1e-5 if what == "norm" else 1e-6
                            pool.wait_ge(var_ready, n)
                            pool.tensor_scalar(vare[:], mv[:, s, :, 1], eps, None, ALU.add).then_inc(pool_step, 1)
                            pool.wait_ge(pool_step, n)
                            pool.tensor_tensor(rstd[:, s], vare[:], c("neg_half"), ALU.pow).then_inc(rstd_ready, 1)
                        if what == "zero":
                            pool.wait_ge(misc_full, count("misc", "cT", s, L))
                            pool.memset(k_ops[:, 1].bitcast(F32), 0.0).then_inc(zeroed, 1)

                @block.tensor
                def _(pe):
                    ident = c("ident")

                    def open_bank(*name):
                        before = PLAN.bank_before[name]
                        if before and before[0] == "misc":
                            pe.wait_ge(misc_done, PLAN.read(*before[:1], *before[1]))
                        elif before and before[0] == "scores":
                            pe.wait_ge(st_done, PLAN.read(*before[:1], *before[1]))
                        elif before:
                            pe.wait_ge(sm_done, PLAN.read(*before[:1], *before[1]))
                        return bank_of(*name)

                    def turn(src, name):
                        bank = open_bank(*name)
                        for t in range(QT):
                            ins = pe.transpose(bank[:, t * P:(t + 1) * P], src[:, t, :], ident)
                        ins.then_inc(misc_full, 1)

                    def rows_out(lhs, w, name):
                        bank = open_bank(*name)
                        n = w.shape[1]
                        for t in range(QT):
                            ins = pe.matmul(bank[:, t * n:(t + 1) * n], lhs[:, t * P:(t + 1) * P], w,
                                            start=True, stop=True, skip_group_check=True)
                        ins.then_inc(misc_full, 1)

                    def columns_out(w, src, name):
                        bank = open_bank(*name)
                        pe.matmul(bank, w, src, start=True, stop=True).then_inc(misc_full, 1)

                    for name in PLAN.order["pe"]:
                        what, s, L = name[:3]
                        kind = LAYERS[L]
                        wsel = ("latent", "ffn", "causal").index(kind)
                        if what in ("v", "pq", "pk", "m1q", "m1k"):
                            pe.wait_ge(misc_done, read("misc", "yT", s, L))
                        if what == "yT":
                            pe.wait_ge(normed, count("applied", "apply", s, L))
                            turn(ys[:, s], name)
                        elif what == "v":
                            rows_out(turned[:, s], w_v[:, wsel, :], name)
                        elif what in ("pq", "pk"):
                            w = wrep[:, (0 if kind == "ffn" else 2) + int(what == "pk"), name[3], :]
                            columns_out(w, turned[:, s], name)
                        elif what in ("m1q", "m1k"):
                            h = GH * name[3] + 2 * name[4]
                            w = w_lat[:, int(what == "m1k"), h:h + 2, :].rearrange("p h l -> p (h l)")
                            columns_out(w, turned[:, s], name)
                        elif what in ("m2q", "m2k"):
                            g, j = name[3:]
                            pe.wait_ge(misc_done, read("misc", "m1" + what[-1], s, L, g, j // 2))
                            lo = 64 * (j % 2)
                            w = w_m2q[:] if what == "m2q" else c("sum3")
                            columns_out(w[lo:lo + 64, :], r1[lo:lo + 64, int(what == "m2k"), :], name)
                        elif what == "max":
                            g, j, qt = name[3:]
                            made = ("m2k", s, L, g, j) if kind == "latent" else ("pk", s, L, g)
                            if kind == "latent":
                                made = max(made, ("m2q", s, L, g, j), key=PLAN.n_read["misc"].get)
                            else:
                                made = max(made, ("pq", s, L, g), key=PLAN.n_read["misc"].get)
                            pe.wait_ge(misc_done, read("misc", *made))
                            q, k = queries(s, L, g, j), keys(s, L, g, j)
                            if kind == "latent":
                                q, k = q[0:96], k[0:96]
                            bank = open_bank(*name)
                            n = T if kind == "ffn" else (qt + 1) * P
                            if kind != "ffn":
                                pe.matmul(bank[:, n - P:n], ident_bf[:], mask_bf[:, 0, :], start=True,
                                          stop=False, skip_group_check=True)
                            pe.matmul(bank[:, 0:n], q[:, qt * P:(qt + 1) * P], k[:, 0:n],
                                      start=(kind == "ffn"), stop=True, skip_group_check=True)\
                                .then_inc(sm_full, 1)
                        elif what == "mT":
                            pe.wait_ge(folded, count("folds", "fold", s, L, name[3]))
                            turn((mx_lat if kind == "latent" else mx[:, s]).bitcast(F32), name)
                        elif what == "st":
                            g, kt, j = name[3:]
                            if kind == "latent":
                                pe.wait_ge(shifted, count("shifts", "mT", s, L, g))
                            else:
                                pe.wait_ge(misc_done, read("misc", "mT", s, L, g))
                            q, k = queries(s, L, g, j), keys(s, L, g, j)
                            bank = open_bank(*name)
                            lo = 0 if kind == "ffn" else kt * P
                            if kind != "ffn":
                                pe.matmul(bank[:, lo:lo + P], ident_bf[:], mask_bf[:, 1, :], start=True,
                                          stop=False, skip_group_check=True)
                            pe.matmul(bank[:, lo:T], k[:, kt * P:(kt + 1) * P], q[:, lo:T],
                                      start=(kind == "ffn"), stop=True, skip_group_check=True)\
                                .then_inc(st_full, 1)
                        elif what == "av":
                            g, kt = name[3:]
                            pe.wait_ge(misc_done, read("misc", "v", s, L))
                            pe.wait_ge(st_done, read("scores", "st", s, L, g, kt, GH - 1))
                            if kt == QT - 1 and NG * L + g > 0:
                                pl, pg = divmod(NG * L + g - 1, NG)
                                pe.wait_ge(o_copied, count("copies", "av", s, pl, pg, 0))
                            lo = 0 if kind == "ffn" else kt * P
                            slot = PLAN.slot[name]
                            for j in range(GH):
                                ins = pe.matmul(ps[32 * j:32 * j + 2 * HD, O_BANK[s], lo:T],
                                                va[:, s, kt, GH * g + j, :], wide[:, slot, j, lo:T],
                                                start=(kt == QT - 1), stop=(kt == 0), skip_group_check=True)
                            ins.then_inc(av_done, 1)
                        elif what == "oT":
                            pe.wait_ge(o_copied, count("copies", "av", s, L, name[3], 0))
                            turn(os_[:, s].rearrange("p (t n) -> p t n", t=QT), name)
                        elif what == "cT":
                            last = max(PLAN.n_read["misc"]["oT", s, L, g] for g in range(NG))
                            pe.wait_ge(misc_done, last + 1)
                            turn(ctxs[:, s], name)
                        elif what == "wo":
                            pe.wait_ge(misc_done, read("misc", "cT", s, L))
                            rows_out(turned[:, s], w_o[:, wsel, :], name)
                        elif what == "zT":
                            pe.wait_ge(z_ready, count("zs", "z", s, L))
                            turn(zs[:, s], name)
                        elif what == "rt":
                            pe.wait_ge(misc_done, read("misc", "zT", s, L))
                            rows_out(turned[:, s], wr_sb[:], name)
                        elif what == "gT":
                            pe.wait_ge(gated, count("gates", "gate", s, L))
                            bank = open_bank(*name)
                            for t in range(QT):
                                ins = pe.transpose(bank[0:E, t * P:(t + 1) * P], gates[:, s, t, :], ident)
                            ins.then_inc(misc_full, 1)
                        elif what == "h":
                            pe.wait_ge(misc_done, read("misc", "zT", s, L))
                            e, ch = name[3:]
                            bank = open_bank(*name)
                            pe.matmul(bank, we1_sb[:, e, ch * P:(ch + 1) * P], turned[:, s],
                                      start=True, stop=True).then_inc(st_full, 1)
                        elif what == "o":
                            e = name[3]
                            pe.wait_ge(st_done, read("scores", "h", s, L, e, FC - 1))
                            bank = open_bank(*name)
                            for t in range(QT):
                                for ch in range(FC):
                                    ins = pe.matmul(bank[:, t * P:(t + 1) * P],
                                                    wide[:, PLAN.slot[name], ch, t * P:(t + 1) * P], we2_sb[:, e, ch, :],
                                                    start=(ch == 0), stop=(ch == FC - 1),
                                                    skip_group_check=True)
                            ins.then_inc(sm_full, 1)
                        elif what == "be2":
                            pe.wait_ge(misc_done, read("misc", "gT", s, L))
                            bank = open_bank(*name)
                            for t in range(QT):
                                ins = pe.matmul(bank[:, t * P:(t + 1) * P],
                                                m_rows[32 * s:32 * s + E, t * P:(t + 1) * P],
                                                be2_sb[32 * s:32 * s + E, :], start=True, stop=True,
                                                skip_group_check=True)
                            ins.then_inc(misc_full, 1)

                @block.scalar
                def _(act):
                    def slot_free(*unit):
                        before = PLAN.before[unit]
                        if before and before[0] == "av":
                            act.wait_ge(av_done, count("values", *before))
                        elif before:
                            act.wait_ge(sm_full, count("smax", *before))

                    for name in PLAN.order["act"]:
                        what, s, L = name[:3]
                        kind = LAYERS[L]
                        scale = LAT ** -0.5 if kind == "latent" else HD ** -0.5
                        if what in ("pq", "pk", "m2q", "m2k"):
                            n = PLAN.n["parts"][name]
                            act.wait_ge(misc_full, count("misc", *name))
                            if n >= 2:
                                act.wait_ge(misc_done, read("misc", *list(PLAN.n["parts"])[n - 2]))
                            bank = bank_of(*name)
                            if what == "m2q":
                                ins = act.activation(part[:, n % 2], bank, ACT.Identity, scale=c("lq_low"),
                                                     bias=bq_m2_low[:])
                            else:
                                rows_low = {"pq": "q_low", "pk": "k_low", "m2k": "lk_low"}[what]
                                ins = act.activation(part[:, n % 2], bank, ACT.Copy, scale=c(rows_low))
                            ins.then_inc(parts, 1)
                        elif what == "st":
                            g, kt, j = name[3:]
                            slot = PLAN.slot["av", s, L, g, kt]
                            if j == 0:
                                slot_free("av", s, L, g, kt)
                            lo = 0 if kind == "ffn" else kt * P
                            act.wait_ge(st_full, count("scores", *name))
                            act.activation(wide[:, slot, j, lo:T], bank_of(*name)[:, lo:T],
                                           ACT.Exp, scale=scale).then_inc(st_done, 1)
                        elif what == "mT":
                            g = name[3]
                            act.wait_ge(misc_done, read("misc", *name))
                            act.copy(q_lat[96:P, g % 2], m_rows[96:P, :].unsqueeze(1).broadcast_to([32, GH, T]))\
                                .then_inc(shifted, 1)
                        elif what == "av" and name[4] == 0:
                            g = name[3]
                            act.wait_ge(av_done, count("values", *name))
                            if NG * L + g > 0:
                                pl, pg = divmod(NG * L + g - 1, NG)
                                act.wait_ge(misc_full, count("misc", "oT", s, pl, pg))
                            act.copy(os_[:, s], ps[:, O_BANK[s], :]).then_inc(o_copied, 1)
                        elif what == "rt":
                            act.wait_ge(logits, count("routes", *name))
                            act.activation(lg[:, s, 1], lg[:, s, 0], ACT.Exp).then_inc(exped, 1)
                        elif what == "top":
                            act.wait_ge(gdiff, count("tops", *name))
                            act.activation(r4[:, s, 3], r4[:, s, 2], ACT.Exp).then_inc(exped, 1)
                        elif what == "h":
                            e, ch = name[3:]
                            if ch == 0:
                                slot_free("o", s, L, e)
                            act.wait_ge(st_full, count("scores", *name))
                            act.activation(wide[:, PLAN.slot["o", s, L, e], ch, :],
                                           bank_of(*name), ACT.Gelu,
                                           bias=be1_sb[:, e * FC + ch:e * FC + ch + 1]).then_inc(st_done, 1)

                @block.vector
                def _(dve):
                    n_step = 0

                    def step(ins):
                        nonlocal n_step
                        n_step += 1
                        ins.then_inc(dve_step, 1)
                        dve.wait_ge(dve_step, n_step)

                    def every_tile(row):
                        return row.unsqueeze(1).broadcast_to([P, QT, P])

                    def stats(s, src):
                        for t in range(QT):
                            ins = dve.bn_stats(st6[:, t, :], src[:, t, :])
                        step(ins)
                        for t in range(QT):
                            ins = dve.bn_aggr(mv[:, s, t, :], st6[:, t, :])
                        ins.then_inc(var_ready, 1)

                    def apply(s, dst, src, name):
                        dve.wait_ge(rstd_ready, count("stats", *name))
                        for t in range(QT):
                            ins = dve.tensor_scalar(dst[:, t, :], src[:, t, :], mv[:, s, t, 0:1],
                                                    rstd[:, s, t:t + 1], ALU.subtract, ALU.mult)
                        return ins

                    def filled(name):
                        dve.wait_ge(misc_full, count("misc", *name))
                        return bank_of(*name)

                    def gained(dst, gain, bias):
                        step(dve.tensor_tensor(dst, dst, every_tile(gain), ALU.mult))
                        return dve.tensor_tensor(dst, dst, every_tile(bias), ALU.add)

                    over = [P, QT, E]

                    dve.wait_ge(x_in, 32)
                    for name in PLAN.order["dve"]:
                        what, s, L = name[:3]
                        kind = LAYERS[L]
                        x_s = xs[:, s]
                        if what == "norm":
                            stats(s, x_s)
                        elif what == "apply":
                            apply(s, ys[:, s], x_s, ("norm", s, L)).then_inc(normed, 1)
                        elif what == "yT":
                            dve.tensor_copy(turned[:, s], filled(name)).then_inc(misc_done, 1)
                        elif what == "v":
                            dve.tensor_copy(va[:, s, :, :, 0:HD],
                                            filled(name).rearrange("p (t h i) -> p t h i", t=QT, h=H))\
                                .then_inc(misc_done, 1)
                        elif what in ("m1q", "m1k"):
                            m, pair = int(what == "m1k"), 2 * name[3] + name[4]
                            if pair > 0:
                                prev = ("m2" + what[-1], s, L, (pair - 1) // 2, 2 * ((pair - 1) % 2) + 1)
                                dve.wait_ge(misc_full, count("misc", *prev))
                            dve.scalar_tensor_tensor(
                                out=r1[:, m, :], in0=filled(name), scalar=b_lat[:, m, pair:pair + 1],
                                in1=c("cos_sin"), op0=ALU.add, op1=ALU.mult).then_inc(misc_done, 1)
                        elif what in ("pq", "pk", "m2q", "m2k"):
                            add = {"pq": c("zero"), "pk": c("k_one"), "m2q": bq_m2[:],
                                   "m2k": c("lk_one")[:, name[-1] % GH:name[-1] % GH + 1]}[what]
                            bank = filled(name)
                            dve.wait_ge(parts, count("parts", *name))
                            high = part[:, PLAN.n["parts"][name] % 2].bitcast(F32)
                            g, j = name[3], name[-1] % GH
                            if g >= 2:
                                dve.wait_ge(st_full, count("scores", "st", s, L, g - 2, 0, GH - 1))
                            if name == ("pk", 1, 1, 0):
                                dve.wait_ge(zeroed, 1)
                            cuts = [(32 * i, 32 * i + 32, keys(s, L, g, i)) for i in range(GH)] if what == "pk" \
                                else [(0, P, keys(s, L, g, j) if what == "m2k" else queries(s, L, g, j))]
                            for lo, hi, dst in cuts:
                                ins = dve.scalar_tensor_tensor(
                                    out=dst[lo:hi], in0=bank[lo:hi], scalar=add[lo:hi], in1=high[lo:hi],
                                    op0=ALU.add, op1=ALU.subtract)
                            ins.then_inc(misc_done, 1)
                        elif what == "max":
                            g, j, qt = name[3:]
                            n = T if kind == "ffn" else (qt + 1) * P
                            if j == 0 and qt == 0 and NG * L + g > 0:
                                pl, pg = divmod(NG * L + g - 1, NG)
                                dve.wait_ge(folded, count("folds", "fold", s, pl, pg))
                            dve.wait_ge(sm_full, count("smax", *name))
                            dve.tensor_reduce(nmax[:, s, j, qt:qt + 1],
                                              bank_of(*name)[:, 0:n], AX.X, ALU.max,
                                              negate=True).then_inc(sm_done, 1)
                        elif what == "fold":
                            g = name[3]
                            dve.wait_ge(sm_done, read("smax", "max", s, L, g, GH - 1, QT - 1))
                            if kind == "latent":
                                cols = mx_lat[:, :, M_ROW_LAT:M_ROW_LAT + 2 * GH]\
                                    .rearrange("p t (j s) -> p j t s", s=2)
                                high, low = cols[:, :, :, 0], cols[:, :, :, 1]
                            else:
                                cols = mx[:, s].rearrange("p t (j s) -> p j t s", s=32)
                                high, low = cols[:, :, :, M_ROW], cols[:, :, :, M_ROW + 1]
                            if g > 0:
                                dve.wait_ge(misc_full, count("misc", "mT", s, L, g - 1))
                            step(dve.tensor_copy(high, nmax[:, s]))
                            dve.tensor_tensor(low, nmax[:, s], high.bitcast(F32), ALU.subtract)\
                                .then_inc(folded, 1)
                        elif what == "mT":
                            g = name[3]
                            bank = filled(name)
                            if kind == "latent":
                                if g >= 1:
                                    dve.wait_ge(shifted, count("shifts", "mT", s, L, g - 1))
                                dve.tensor_copy(m_rows[96:P, :], bank[96:P, :]).then_inc(misc_done, 1)
                            else:
                                dst = queries(s, L, g, 0)
                                dve.wait_ge(misc_done, read("misc", "pq", s, L, g))
                                dve.tensor_tensor(dst, bank, dst.bitcast(F32), ALU.add).then_inc(misc_done, 1)
                        elif what == "oT":
                            g = name[3]
                            bank = filled(name).rearrange("p (t j s) -> p t j s", t=QT, s=32)
                            if PLAN.n_read["misc"][name]:
                                dve.wait_ge(misc_done, PLAN.n_read["misc"][name])
                            step(dve.reciprocal(rden[:], bank[:, :, :, HD]))
                            dve.tensor_tensor(
                                ctxs[:, s, :, g * 32:(g + 1) * 32].rearrange("p t (j i) -> p t j i", i=HD),
                                bank[:, :, :, 0:HD], rden[:].unsqueeze(3).broadcast_to([P, QT, GH, HD]),
                                ALU.mult).then_inc(misc_done, 1)
                        elif what in ("cT", "zT"):
                            dve.tensor_copy(turned[:, s], filled(name)).then_inc(misc_done, 1)
                        elif what == "gT":
                            dve.tensor_copy(m_rows[32 * s:32 * s + E, :], filled(name)[0:E, :])\
                                .then_inc(misc_done, 1)
                        elif what == "wo":
                            bank = filled(name).rearrange("p (t d) -> p t d", t=QT)
                            old, dst = (ys[:, s], ctxs[:, s]) if kind == "ffn" else (x_s, x_s)
                            dve.tensor_tensor(dst, bank, old, ALU.add).then_inc(misc_done, 1)
                            dve.wait_ge(misc_done, read("misc", *name))
                            if kind == "latent":
                                step(dve.tensor_tensor(x_s, x_s, every_tile(bias_lat[:]), ALU.add))
                            if kind == "ffn":
                                step(dve.tensor_tensor(dst, dst, every_tile(rows[:, 0, :]), ALU.add))
                                stats(s, dst)
                        elif what == "z":
                            step(apply(s, zs[:, s], ctxs[:, s], ("wo", s, L)))
                            gained(zs[:, s], rows[:, 1, :], rows[:, 2, :]).then_inc(z_ready, 1)
                        elif what == "rt":
                            bank = filled(name)[:, 0:QT * E].rearrange("p (t e) -> p t e", t=QT)
                            step(dve.tensor_reduce(r4[:, s, 0], bank, AX.X, ALU.max))
                            dve.tensor_tensor(lg[:, s, 0], bank, r4[:, s, 0].unsqueeze(2).broadcast_to(over),
                                              ALU.subtract).then_inc(misc_done, 1)
                            dve.wait_ge(misc_done, read("misc", *name))
                            dve.nop().then_inc(logits, 1)
                        elif what == "top":
                            r, l = r4[:, s], lg[:, s]
                            dve.wait_ge(exped, count("exps", "rt", s, L))
                            step(dve.tensor_reduce(r[:, 1], l[:, 1], AX.X, ALU.add))
                            step(dve.reciprocal(r[:, 1], r[:, 1]))
                            step(dve.tensor_tensor(l[:, 2], l[:, 1], r[:, 1].unsqueeze(2).broadcast_to(over),
                                                   ALU.mult))
                            for t in range(QT):
                                ins = dve.max(l[:, 3, t, :], l[:, 2, t, :])
                            step(ins)
                            for t in range(QT):
                                ins = dve.max_index(lgi[:, s, t, :], l[:, 3, t, :], l[:, 2, t, :])
                            step(ins)
                            dve.tensor_tensor(r[:, 2], l[:, 3, :, 1], l[:, 3, :, 0], ALU.subtract)\
                                .then_inc(gdiff, 1)
                        elif what == "gate":
                            r, l = r4[:, s], lg[:, s]
                            step(dve.tensor_copy(lgf[:], lgi[:, s]))
                            dve.wait_ge(exped, count("exps", "top", s, L))
                            step(dve.tensor_scalar(r[:, 4], r[:, 3], 1.0, None, ALU.add))
                            step(dve.reciprocal(r[:, 4], r[:, 4]))
                            step(dve.tensor_tensor(r[:, 5], r[:, 3], r[:, 4], ALU.mult))
                            which = c("expert").unsqueeze(1).broadcast_to(over)
                            for n in range(2):
                                ins = dve.tensor_tensor(l[:, 3 + n], which,
                                                        lgf[:, :, n:n + 1].broadcast_to(over), ALU.is_equal)
                            step(ins)
                            for n in range(2):
                                ins = dve.tensor_tensor(l[:, 3 + n], l[:, 3 + n],
                                                        r[:, 4 + n].unsqueeze(2).broadcast_to(over), ALU.mult)
                            step(ins)
                            dve.tensor_tensor(gates[:, s], l[:, 3], l[:, 4], ALU.add).then_inc(gated, 1)
                        elif what == "o":
                            e = name[3]
                            if e == 0:
                                dve.wait_ge(gated, count("gates", "gate", s, L))
                            dve.wait_ge(sm_full, count("smax", *name))
                            bank = bank_of(*name).rearrange("p (t d) -> p t d", t=QT)
                            dst = ctxs[:, s] if e == 0 else tmp[:]
                            dve.tensor_tensor(dst, bank, gates[:, s, :, e:e + 1].broadcast_to([P, QT, P]),
                                              ALU.mult).then_inc(sm_done, 1)
                            dve.wait_ge(sm_done, read("smax", *name))
                            if e > 0:
                                step(dve.tensor_tensor(ctxs[:, s], ctxs[:, s], tmp[:], ALU.add))
                        elif what == "be2":
                            bank = filled(name).rearrange("p (t d) -> p t d", t=QT)
                            total = ctxs[:, s]
                            dve.tensor_tensor(total, bank, total, ALU.add).then_inc(misc_done, 1)
                            dve.wait_ge(misc_done, read("misc", *name))
                            step(dve.tensor_tensor(total, total, zs[:, s], ALU.add))
                            stats(s, total)
                        elif what == "end" and kind == "ffn":
                            total = ctxs[:, s]
                            step(apply(s, total, total, ("be2", s, L)))
                            step(gained(total, rows[:, 3, :], rows[:, 4, :]))
                            ins = dve.tensor_tensor(x_s, x_s, total, ALU.add)
                            if L == LAST:
                                ins.then_inc(seq_done, 1)
                            else:
                                step(ins)

            nc.all_engine_barrier()
            for s in turn_sems:
                nc.gpsimd.sem_clear(s)
            nc.all_engine_barrier()


PREP_REP = 8 + 5 + 3 + 6
PREP_BLOCKD = PREP_REP + 2 + 6 + 2 + 1
PREP_OUT = PREP_BLOCKD - 1 + 6 + 3 + 3

_INS = ["L0_attn_a_x", "L0_attn_a_c_attn_w", "L0_attn_a_c_attn_b", "L0_attn_a_q2l_w", "L0_attn_a_q2l_b",
        "L0_attn_a_kv2l_w", "L0_attn_a_kv2l_b", "L0_attn_a_l2o_w", "L0_attn_a_l2o_b", "L0_attn_a_wqk_w",
        "L0_attn_a_wqk_b", "L0_attn_a_cproj_w", "L0_attn_a_cproj_b", "L0_attn_b_w_qkv", "L0_attn_b_w_o",
        "L0_ffn_Wq", "L0_ffn_Wk", "L0_ffn_Wv", "L0_ffn_Wo", "L0_ffn_bo", "L0_ffn_Wr", "L0_ffn_We1",
        "L0_ffn_be1", "L0_ffn_We2", "L0_ffn_be2", "L0_ffn_ln1_g", "L0_ffn_ln1_b", "L0_ffn_ln2_g",
        "L0_ffn_ln2_b"]


def kernel(**inputs):
    import concourse.bacc as bacc
    from concourse.bass_utils import run_bass_kernel_spmd

    nc = bacc.Bacc("TRN2", target_bir_lowering=False, num_devices=1)
    arrays, args = {}, []
    for name in _INS:
        a = np.ascontiguousarray(inputs[name])
        arrays[name + "_dram"] = a
        args.append(nc.dram_tensor(name + "_dram", a.shape, mybir.dt.from_np(a.dtype), kind="ExternalInput").ap())
    arrays["const_dram"] = CONST
    args.append(nc.dram_tensor("const_dram", CONST.shape, F32, kind="ExternalInput").ap())
    args.append(nc.dram_tensor("out_dram", (4, T, P), F32, kind="ExternalOutput").ap())
    hybrid_kernel(nc, *args)
    r = run_bass_kernel_spmd(nc, [arrays], core_ids=[0])
    return r.results[0]["out_dram"]
```

```python
from contextlib import ExitStack

import numpy as np

import concourse.bass as bass
from concourse import mybir
from concourse.alu_op_type import AluOpType as ALU

ACT = mybir.ActivationFunctionType
AX = mybir.AxisListType
F32 = mybir.dt.float32
F32R = mybir.dt.float32r
BF16 = mybir.dt.bfloat16
U32 = mybir.dt.uint32

P = 128
T = 512
QT = T // P
H = 16
HD = 8
LAT = 32
GH = 4
NG = H // GH
E = 8
FC = 4
NEG = -1e30
LAYERS = ("latent", "ffn", "causal", "ffn")
M_ROW = 24
LEAD, GRAIN, SWITCH = 50000, 1, 500
SOON = {}
M_ROW_LAT = 96


def constants():
    cols, at, n = [], {}, 0

    def put(name, a):
        nonlocal n
        full = np.zeros((P, a.shape[1]), np.float32)
        full[: a.shape[0]] = a
        cols.append(full)
        at[name] = (n, n + a.shape[1])
        n += a.shape[1]

    eye = np.eye(P, dtype=np.float32)
    i = np.arange(P)
    put("ident", eye)
    put("mask_qk", np.where(i[None, :] > i[:, None], np.float32(NEG), np.float32(0)))
    put("mask_kq", np.where(i[:, None] > i[None, :], np.float32(NEG), np.float32(0)))
    exponent = np.arange(0, LAT, 2, dtype=np.float32) / np.float32(LAT)
    inv = (np.float32(1.0) / np.power(np.float32(10000.0), exponent)).astype(np.float32)
    freqs = np.outer(np.arange(T, dtype=np.float32), inv).astype(np.float32)
    cos = np.repeat(np.cos(freqs), 2, axis=1).T.astype(np.float32)
    sin = np.repeat(np.sin(freqs), 2, axis=1).T.astype(np.float32)
    put("cos_sin", np.concatenate([cos, sin, cos, sin]))
    put("own_head", (i[:, None] // HD == np.arange(H)[None, :]).astype(np.float32))
    i32 = np.eye(LAT, dtype=np.float32)
    rot_t = np.zeros((LAT, LAT), np.float32)
    for k in range(0, LAT, 2):
        rot_t[k + 1, k] = -1.0
        rot_t[k, k + 1] = 1.0
    put("sum3", np.tile(np.concatenate([i32, i32, i32, np.zeros_like(i32)], 1), (4, 1)))
    s = i % 32
    put("q_low", ((s >= 8) & (s < 16)).astype(np.float32)[:, None])
    put("k_low", ((s >= 16) & (s < 24)).astype(np.float32)[:, None])
    put("k_one", ((s == M_ROW) | (s == M_ROW + 1)).astype(np.float32)[:, None])
    put("lq_low", ((i >= 32) & (i < 64)).astype(np.float32)[:, None])
    put("lk_low", ((i >= 64) & (i < 96)).astype(np.float32)[:, None])
    put("lk_one", np.stack([(i - M_ROW_LAT) // 2 == j for j in range(GH)], 1).astype(np.float32))
    put("zero", np.zeros((P, 1), np.float32))
    put("expert", np.tile(np.arange(E, dtype=np.float32)[None], (P, 1)))
    put("neg_half", np.full((P, QT), -0.5, np.float32))
    put("eye_rot", np.concatenate([i32, rot_t], 1))
    put("eye_rot2", np.concatenate([i32, rot_t, i32, rot_t], 1))
    put("eye4", np.tile(i32, (1, 4)))
    return np.concatenate(cols, 1), at


CONST, CONST_AT = constants()


PASS, TURN, ROWS = 216, 430, 880
LATENCY = {"pe": 200, "dve": 180, "act": 220, "pool": 160}
SPREAD = 4 * 480
TABLE = 1300


def sequence_tasks(s):
    t = {}

    def add(eng, name, ns, *before):
        t[eng, name] = (ns, [b for b in before if b is not None])

    for L, kind in enumerate(LAYERS):
        def span(n):
            return PASS * n // QT + (60 if kind != "ffn" else 0)

        here = (s, L)
        last = [("dve", ("end", s, L - 1))] if L else []
        add("dve", ("norm", *here), 1450, *last)
        add("pool", ("norm", *here), 1150, ("dve", ("norm", *here)))
        add("dve", ("apply", *here), 1030, ("pool", ("norm", *here)))
        add("pe", ("yT", *here), TURN, ("dve", ("apply", *here)))
        add("act", ("yT", *here), 480, ("pe", ("yT", *here)))
        add("pe", ("v", *here), ROWS, ("act", ("yT", *here)))
        add("act", ("v", *here), 480, ("pe", ("v", *here)))
        for g in range(NG):
            used = ("pe", ("st", s, L, g - 2, 0, GH - 1)) if g >= 2 else None
            if kind != "latent":
                for n, free in (("pq", used), ("pk", ("act", ("spread", s, L, g - 1)) if g else None)):
                    name = (n, s, L, g)
                    add("pe", name, 4 * PASS, ("act", ("yT", *here)), ("pe", ("pk", s, L, g - 1)) if g else None)
                    add("act", name, 575, ("pe", name))
                    add("dve", name, 663, ("act", name), free)
                add("act", ("spread", s, L, g), SPREAD, ("dve", ("pk", s, L, g)), used)
            else:
                for j in range(GH):
                    for m in "qk":
                        one, two = ("m1" + m, s, L, g, j // 2), ("m2" + m, s, L, g, j)
                        if j % 2 == 0:
                            p = 2 * g + j // 2 - 1
                            prev = ("pe", ("m2" + m, s, L, p // 2, 2 * (p % 2) + 1)) if p >= 0 else None
                            add("pe", one, 4 * PASS, ("act", ("yT", *here)), prev)
                            add("dve", one, 663, ("pe", one), prev)
                        before = ("pe", ("m2" + m, s, L, g, j - 1)) if j % 2 else None
                        add("pe", two, 4 * PASS, ("dve", one), before)
                        add("act", two, 620, ("pe", two))
                        add("dve", two, 663, ("act", two), used)
            for j in range(GH):
                for qt in range(QT):
                    n = QT if kind == "ffn" else qt + 1
                    name = ("max", s, L, g, j, qt)
                    made = [("m2q", s, L, g, j), ("m2k", s, L, g, j)] if kind == "latent" else \
                        [("pq", s, L, g)]
                    k = QT * j + qt - 1
                    order = ("pe", ("max", s, L, g, k // QT, k % QT)) if k >= 0 else None
                    add("pe", name, span(n), *(("dve", x) for x in made), order,
                        ("act", ("spread", s, L, g)) if kind != "latent" else None)
                    add("dve", name, 65 + 133 * n, ("pe", name), ("dve", ("fold", s, L, g - 1)) if g else None,
                        ("dve", order[1]) if order else None)
            fold, up = ("fold", s, L, g), ("mT", s, L, g)
            add("dve", fold, 300, ("dve", ("max", s, L, g, GH - 1, QT - 1)), ("pe", ("mT", s, L, g - 1)) if g else None)
            add("pe", up, TURN, ("dve", fold))
            add("dve", up, 600, ("pe", up), ("act", ("mT", s, L, g - 1)) if g and kind == "latent" else None)
            if kind == "latent":
                add("act", up, 1900, ("dve", up))
            shifted = ("act" if kind == "latent" else "dve", up)
            order = ("pe", ("st", s, L, g - 1, 0, GH - 1)) if g else None
            for kt in reversed(range(QT)):
                w = QT if kind == "ffn" else QT - kt
                for j in range(GH):
                    name = ("st", s, L, g, kt, j)
                    add("pe", name, span(w), shifted, order)
                    add("act", name, 50 + 107 * w, ("pe", name), ("act", order[1]) if order else None)
                    order = ("pe", name)
                name = ("av", s, L, g, kt)
                prev = ("pe", ("av", s, L, g, kt + 1)) if kt < QT - 1 else \
                    ("pe", ("av", s, L, g - 1, 0)) if g else None
                add("pe", name, 4 * PASS * w // QT + 60, ("act", ("v", *here)), ("act", ("st", s, L, g, kt, GH - 1)), prev)
            add("act", ("av", s, L, g, 0), 480, ("pe", ("av", s, L, g, 0)), ("pe", ("oT", s, L, g - 1)) if g else None)
            add("pe", ("oT", s, L, g), TURN, ("act", ("av", s, L, g, 0)))
            add("dve", ("oT", s, L, g), 500, ("pe", ("oT", s, L, g)))
        add("pe", ("cT", *here), TURN, *(("dve", ("oT", s, L, g)) for g in range(NG)))
        add("act", ("cT", *here), 480, ("pe", ("cT", *here)))
        add("pe", ("wo", *here), ROWS, ("act", ("cT", *here)))
        if kind != "ffn":
            add("dve", ("wo", *here), 1400 if kind == "latent" else 700, ("pe", ("wo", *here)))
            if kind == "latent" and s == 1:
                add("pool", ("zero", *here), 3500, ("pe", ("cT", *here)))
            add("dve", ("end", *here), 0, ("dve", ("wo", *here)))
            continue
        add("dve", ("wo", *here), 2900, ("pe", ("wo", *here)))
        add("pool", ("wo", *here), 1150, ("dve", ("wo", *here)))
        add("dve", ("z", *here), 2500, ("pool", ("wo", *here)))
        add("pe", ("zT", *here), TURN, ("dve", ("z", *here)))
        add("act", ("zT", *here), 480, ("pe", ("zT", *here)))
        add("act", ("split", *here), 480, ("act", ("zT", *here)))
        add("dve", ("split", *here), 663, ("act", ("split", *here)))
        add("pe", ("rt", *here), 430, ("act", ("zT", *here)))
        add("dve", ("rt", *here), 400, ("pe", ("rt", *here)))
        add("act", ("rt", *here), 150, ("dve", ("rt", *here)))
        add("dve", ("top", *here), 1800, ("act", ("rt", *here)))
        add("act", ("top", *here), 120, ("dve", ("top", *here)))
        add("dve", ("gate", *here), 1600, ("act", ("top", *here)))
        add("pe", ("gT", *here), TURN, ("dve", ("gate", *here)))
        add("act", ("gT", *here), 480, ("pe", ("gT", *here)))
        add("pe", ("be2", *here), ROWS, ("act", ("gT", *here)))
        add("dve", ("be2", *here), 610, ("pe", ("be2", *here)))
        for e in range(E):
            for ch in range(FC):
                h = ("h", s, L, e, ch)
                k = FC * e + ch - 1
                add("pe", h, 3 * PASS, ("dve", ("split", *here)), ("pe", ("h", s, L, k // FC, k % FC)) if k >= 0 else None)
                add("act", h, 575, ("pe", h), ("act", ("h", s, L, k // FC, k % FC)) if k >= 0 else None)
            o = ("o", s, L, e)
            add("pe", o, 16 * PASS, ("act", h), ("pe", ("o", s, L, e - 1)) if e else None)
            add("dve", o, 1060, ("pe", o), ("dve", ("o", s, L, e - 1) if e else ("be2", *here)))
        add("dve", ("sum", *here), 1450, ("dve", o))
        add("pool", ("sum", *here), 1150, ("dve", ("sum", *here)))
        add("dve", ("end", *here), 3250, ("pool", ("sum", *here)))
    return t


class Plan:

    RINGS = {"misc": ("pq", "pk", "m1q", "m1k", "m2q", "m2k", "mT", "oT", "wo", "rt", "be2"),
             "scores": ("st", "h", "yT", "v", "cT", "zT", "gT"), "smax": ("max", "o")}
    COUNTED = {"values": ("pe", ("av",)), "copies": ("act", ("av",)), "parts": ("act", ("pq", "pk", "m2q", "m2k")),
               "stats": ("dve", ("norm", "wo", "sum")), "applied": ("dve", ("apply",)),
               "folds": ("dve", ("fold",)), "shifts": ("act", ("mT",)), "spreads": ("act", ("spread",)), "zs": ("dve", ("z",)), "z_highs": ("act", ("split",)), "z_lows": ("dve", ("split",)),
               "routes": ("dve", ("rt",)), "tops": ("dve", ("top",)), "gates": ("dve", ("gate",)),
               "exps": ("act", ("rt", "top"))}
    BANKS = 8
    SLOTS = 3

    def __init__(self, lead=LEAD, grain=GRAIN, switch=SWITCH, soon=SOON):
        tasks = {}
        for s in range(2):
            tasks.update(sequence_tasks(s))
        ns, before = tasks["dve", ("norm", 1, 0)]
        tasks["dve", ("norm", 1, 0)] = (ns, before + [("dve", ("oT", 0, 0, NG - 1))])
        ns, before = tasks["act", ("spread", 1, 1, 0)]
        tasks["act", ("spread", 1, 1, 0)] = (ns, before + [("pool", ("zero", 1, 0))])
        reader = {"misc": "dve", "scores": "act", "smax": "dve"}
        for (eng, name), (ns, before) in list(tasks.items()):
            ring = next((r for r, members in self.RINGS.items() if name[0] in members), None)
            if eng == "pe" and ring:
                more = [x for x in tasks[reader[ring], name][1] if x[1][0] != name[0]]
                tasks[eng, name] = (ns, before + more)
        after = {k: [] for k in tasks}
        for k, (_, before) in tasks.items():
            for x in before:
                after[x].append(k)
        rank, open_ = {}, {k: len(v) for k, v in after.items()}
        stack = [k for k, n in open_.items() if n == 0]
        while stack:
            k = stack.pop()
            rank[k] = tasks[k][0] + max((rank[a] + LATENCY[k[0]] for a in after[k]), default=0)
            for x in tasks[k][1]:
                open_[x] -= 1
                if open_[x] == 0:
                    stack.append(x)
        self.order = {"pe": [], "dve": [], "act": [], "pool": []}
        self.n = {r: {} for r in (*self.RINGS, *self.COUNTED)}
        self.n_read = {r: {} for r in self.RINGS}
        self.slot, self.before, self.bank, self.bank_before = {}, {}, {}, {}
        end, clock = {}, dict.fromkeys(self.order, 0)
        banks, filled = [(0, n) for n in range(self.BANKS)], {}
        table, last = "exp", None
        free, owner = [(0, n) for n in range(self.SLOTS)], {}
        missing = {k: len(v[1]) for k, v in tasks.items()}
        ready = [k for k, n in missing.items() if n == 0]
        while ready:
            best = None
            for k in ready:
                eng, name = k
                what = name[0]
                start = max([clock[eng]] + [end[x] + LATENCY[x[0]] for x in tasks[k][1]])
                ring = next((r for r, members in self.RINGS.items() if what in members), None)
                opens = eng == "pe" and (ring or what == "av" and name[4] == QT - 1)
                if opens:
                    if not banks:
                        continue
                    start = max(start, min(banks)[0])
                if eng == "act" and what in ("pq", "pk", "m2q", "m2k"):
                    before = list(self.n["parts"])[-2:]
                    if len(before) == 2:
                        if ("dve", before[0]) not in end:
                            continue
                        start = max(start, end["dve", before[0]] + LATENCY["dve"])
                done = sum(x[0] in ("norm", "wo", "sum") for x in self.order["pool"])
                if eng == "pool" and what in ("norm", "wo", "sum") and \
                        list(self.n["stats"])[done:done + 1] != [name]:
                    continue
                if eng == "pe" and what in ("st", "h") and name[-1] == 0:
                    if not free:
                        continue
                    start = max(start, min(free)[0])
                if what in ("st", "rt", "top", "h") and eng == "act" and (what == "h") != (table == "gelu"):
                    start += TABLE
                wait = start
                if eng == "pe" and what in ("st", "h") and last not in (what, None):
                    wait += switch
                key = (wait // grain, -rank[k] - (lead if name[1] == 0 else 0) - soon.get(what, 0))
                if best is None or key < best[0]:
                    best = (key, k, start, ring, opens)
            assert best, "the tasks wait for each other"
            _, k, start, ring, opens = best
            eng, name = k
            what = name[0]
            ready.remove(k)
            end[k] = clock[eng] = start + tasks[k][0]
            self.order[eng].append(name)
            if what in ("st", "rt", "top", "h") and eng == "act":
                table = "gelu" if what == "h" else "exp"
            if eng == "pe" and what in ("st", "h"):
                last = what
            if ring and eng == "pe":
                self.add(ring, name)
            if opens:
                banks.sort()
                self.bank[name] = banks.pop(0)[1]
                self.bank_before[name] = filled.get(self.bank[name])
                filled[self.bank[name]] = (ring, name) if ring else ("copies", (*name[:4], 0))
            if ring and eng == reader[ring]:
                self.n_read[ring][name] = len(self.n_read[ring])
            if eng == "act" and what == "av":
                banks.append((end[k] + LATENCY[eng], self.bank[(*name[:4], QT - 1)]))
            elif k == ("dve", name) and what == "split":
                banks.append((end[k] + LATENCY[eng], self.bank["zT", *name[1:]]))
            elif ring and eng == reader[ring] and what != "zT":
                banks.append((end[k] + LATENCY[eng], self.bank[name]))
            for count, (who, members) in self.COUNTED.items():
                if eng == who and what in members:
                    if count == "copies" and name[4] or count == "stats" and what != "norm" and \
                            LAYERS[name[2]] != "ffn":
                        continue
                    self.add(count, name)
            if eng == "pe" and what in ("st", "h") and name[-1] == 0:
                unit = ("av" if what == "st" else "o", *name[1:-1])
                free.sort()
                self.slot[unit] = free.pop(0)[1]
                self.before[unit] = owner.get(self.slot[unit])
                owner[self.slot[unit]] = unit
            if eng == "pe" and what in ("av", "o"):
                free.append((end[k] + LATENCY["pe"], self.slot[name]))
            for a in after[k]:
                missing[a] -= 1
                if missing[a] == 0:
                    ready.append(a)
        assert len(end) == len(tasks)
        self.length = max(end.values())

    def add(self, ring, name):
        self.n[ring][name] = len(self.n[ring])

    def count(self, ring, *name):
        return self.n[ring][name] + 1

    def read(self, ring, *name):
        return self.n_read[ring][name] + 1


PLAN = Plan()


def hybrid_kernel(nc, x, wa, ba, q2l, q2lb, kv2l, kv2lb, l2o, l2ob, wqk, wqkb, cproj, cprojb,
                  wqkv, wo_b, wq, wk, wv, wo, bo, wr, we1, be1, we2, be2, g1, b1, g2, b2, const, out):
    with ExitStack() as ctx:
        def sb(name, shape, dt=F32):
            return ctx.enter_context(nc.sbuf_tensor(name, shape, dt))

        def sem(name):
            return ctx.enter_context(nc.semaphore(name))

        ps = ctx.enter_context(nc.psum_tensor("ps", [P, 8, T], F32))

        cst = sb("cst", [P, CONST.shape[1]])
        ident_bf = sb("ident_bf", [P, P], BF16)
        mask_bf = sb("mask_bf", [P, 2, P], BF16)
        small = sb("small", [P, 128])
        wrep = sb("wrep", [P, 4, NG, P])
        w_v = sb("w_v", [P, 3, P])
        w_o = sb("w_o", [P, 3, P])
        w_lat = sb("w_lat", [P, 2, H, 2 * LAT])
        b_lat = sb("b_lat", [P, 2, H // 2])
        w_m2q = sb("w_m2q", [P, P])
        bq_m2 = sb("bq_m2", [P, 1])
        bq_m2_low = sb("bq_m2_low", [P, 1])
        cvec = sb("cvec", [P, 1])
        bias_lat = sb("bias_lat", [P, P])
        rows = sb("rows", [P, 6, P])
        wr_sb = sb("wr_sb", [P, E])
        we1_parts = sb("we1_parts", [P, 2, E, FC * P], F32R)
        we2_sb = sb("we2_sb", [P, E, FC, P])
        be1_sb = sb("be1_sb", [P, E * FC])
        be2_sb = sb("be2_sb", [P, P])
        xs = sb("xs", [P, 2, QT, P])
        ys = sb("ys", [P, 2, QT, P])
        turned = sb("turned", [P, 2, T])
        va = sb("va", [P, 2, QT, H, 2 * HD])
        os_ = sb("os_", [P, 2, T])
        ctxs = sb("ctxs", [P, 2, QT, P])
        gates = sb("gates", [P, 2, QT, E])
        q_x = sb("q_x", [P, 2, T], F32R)
        k_ops = sb("k_ops", [P, 2, 2, GH, T], F32R)
        nmax = sb("nmax", [P, 2, GH, QT])
        mx = sb("mx", [P, 2, QT, P], F32R)
        mx_lat = sb("mx_lat", [P, QT, P], F32R)
        q_lat = sb("q_lat", [P, 2, GH, T], F32R)
        m_rows = sb("m_rows", [P, T])
        k_all = sb("k_all", [P, 2, T], F32R)
        part = sb("part", [P, 2, T], F32R)
        r1 = sb("r1", [P, 2, T])
        wide = sb("wide", [P, Plan.SLOTS, GH, T])
        tmp, cprojT, bcast = ctxs[:, 0], ys[:, 0, 0, :], ys[:, 0, 1:3, :]
        rden = sb("rden", [P, QT, GH])
        st6 = sb("st6", [P, QT, 6])
        vare = sb("vare", [P, 2, QT])
        mv = sb("mv", [P, 2, QT, 2])
        rstd = sb("rstd", [P, 2, QT])
        lg = sb("lg", [P, 2, 5, QT, E])
        lgi = sb("lgi", [P, 2, QT, E], U32)
        lgf = sb("lgf", [P, QT, E])
        r4 = sb("r4", [P, 2, 6, QT])

        raw = wide[:].rearrange("p e c n -> p (e c n)")[:, 0:9 * P].rearrange("p (m n) -> p m n", n=P)
        blockd = r1[:].rearrange("p m (h l) -> p (m h) l", l=2 * LAT)

        we1_raw = wide[:].rearrange("p e c n -> p (e c n)")[:, 9 * P:9 * P + E * FC * P]

        def c(name):
            a, b = CONST_AT[name]
            return cst[:, a:b]

        loaded = sem("loaded")
        loaded_small = sem("loaded_small")
        loaded_late = sem("loaded_late")
        we1_in = sem("we1_in")
        we1_high = sem("we1_high")
        prep_pe = sem("prep_pe")
        prep_dve = sem("prep_dve")

        with nc.Block() as block:
            n_loads = {loaded: 0, loaded_small: 0, loaded_late: 0}

            def load(queue, dst, src, signal):
                n_loads[signal] += 16
                queue.dma_start(dst, src, allow_slow_non_contiguous=True).then_inc(signal, 16)

            @block.sync
            def _(sp):
                def every_partition(a, n, p=P):
                    return a.rearrange("(o n) -> o n", o=1).broadcast_to([p, n])

                load(sp, cst[:], const, loaded)
                load(sp, raw[:, 0:3, :], wa.rearrange("(s o) d -> o s d", s=3), loaded)
                load(sp, raw[:, 3, :], cproj, loaded)
                load(sp, raw[:, 4:7, :], wqkv.rearrange("s h k m -> (h k) s m"), loaded)
                load(sp, raw[:, 7, :], wo_b, loaded)
                load(sp, small[0:LAT, 4:12], q2l, loaded)
                load(sp, small[0:LAT, 12:20], kv2l, loaded)
                load(sp, small[0:LAT, 24:32], l2o.rearrange("o l -> l o"), loaded)
                load(sp, raw[:, 8, :], wq, loaded)
                load(sp, bcast[:, 0, :], wk, loaded)
                load(sp, small[0:LAT, 32:64], wqk.rearrange("o l -> l o"), loaded)
                load(sp, rows[:, 5, :], every_partition(cprojb, P), loaded)
                sp.dma_start(we1_raw, we1.rearrange("e d f -> d e f")).then_inc(we1_in, 16)
                load(sp, w_v[:, 1, :], wv, loaded_late)
                load(sp, w_o[:, 1, :], wo, loaded_late)
                for r, a in enumerate((bo, g1, b1, g2, b2)):
                    load(sp, rows[:, r, :], every_partition(a, P), loaded_late)
                load(sp, wr_sb[:], wr, loaded_late)
                load(sp, be1_sb[:], be1.rearrange("e (c p) -> p (e c)", p=P), loaded_late)
                load(sp, be2_sb[0:E, :], be2, loaded_late)
                load(sp, be2_sb[32:32 + E, :], be2, loaded_late)
                load(sp, we2_sb[:], we2.rearrange("e (c p) d -> p e c d", p=P), loaded_late)
                sp.wait_ge(loaded_late, n_loads[loaded_late])

            @block.gpsimd
            def _(pool):
                load(pool, small[:, 0:3], ba.rearrange("(s o) -> o s", s=3), loaded_small)
                load(pool, small[0:LAT, 20:21], q2lb.rearrange("(n o) -> n o", o=1), loaded_small)
                load(pool, small[0:LAT, 21:22], kv2lb.rearrange("(n o) -> n o", o=1), loaded_small)
                for r in range(3):
                    load(pool, small[r * LAT:(r + 1) * LAT, 64:65], wqkb.rearrange("(n o) -> n o", o=1), loaded_small)
                for h in range(H):
                    load(pool, small[h * HD:(h + 1) * HD, 65:66], l2ob.rearrange("(n o) -> n o", o=1), loaded_small)

            @block.scalar
            def _(act):
                act.wait_ge(we1_in, 16)
                act.copy(we1_parts[:, 0].rearrange("p e n -> p (e n)"), we1_raw).then_inc(we1_high, 1)

            @block.vector
            def _(dve):
                done = [0]

                def step(ins):
                    done[0] += 1
                    ins.then_inc(prep_dve, 1)
                    dve.wait_ge(prep_dve, done[0])

                step(dve.memset(va[:], 1.0))
                step(dve.memset(ps[:], 0.0))
                step(dve.memset(w_m2q[:], 0.0))
                step(dve.memset(wrep[:], 0.0))
                step(dve.memset(bq_m2[:], 0.0))
                step(dve.memset(mx[:].bitcast(F32), 0.0))
                step(dve.memset(mx_lat[:].bitcast(F32), 0.0))
                step(dve.memset(k_ops[:, 0].bitcast(F32), 0.0))
                dve.wait_ge(loaded, n_loads[loaded])
                dve.wait_ge(loaded_small, n_loads[loaded_small])
                step(dve.tensor_copy(ident_bf[:], c("ident")))
                step(dve.tensor_copy(mask_bf[:, 0, :], c("mask_qk")))
                step(dve.tensor_copy(mask_bf[:, 1, :], c("mask_kq")))
                step(dve.tensor_copy(bq_m2[0:96, :], small[0:96, 64:65]))
                step(dve.tensor_tensor(bq_m2_low[:], bq_m2[:], c("lq_low"), ALU.mult))
                for n, col in enumerate((4, 12, 24)):
                    step(dve.tensor_copy(tmp[0:LAT, n, :].rearrange("p (h i) -> p h i", h=H),
                                         small[0:LAT, col:col + HD].unsqueeze(1).broadcast_to([LAT, H, HD])))
                for m, src in enumerate((raw[:, 8, :], bcast[:, 0, :])):
                    for r in range(3):
                        step(dve.tensor_copy(
                            wrep[:, m].rearrange("p g (j s) -> p (g j) s", j=GH)[:, :, 8 * r:8 * r + 8],
                            src.rearrange("p (h i) -> p h i", h=H)))
                ready = done[0]
                assert ready == PREP_REP
                dve.wait_ge(prep_pe, 1)
                step(dve.tensor_copy(w_v[:, 0, :], ps[:, 0, 0:P]))
                step(dve.tensor_copy(cprojT[:], ps[:, 0, P:2 * P]))
                for m in range(2):
                    for r in range(3):
                        step(dve.tensor_copy(
                            wrep[:, 2 + m].rearrange("p g (j s) -> p (g j) s", j=GH)[:, :, 8 * r:8 * r + 8],
                            ps[:, 0, (2 + m) * P:(3 + m) * P].rearrange("p (h i) -> p h i", h=H)))
                step(dve.tensor_copy(w_v[:, 2, :], ps[:, 1, 0:P]))
                step(dve.tensor_copy(w_o[:, 2, :], ps[:, 1, P:2 * P]))
                for m in range(2):
                    dve.wait_ge(prep_pe, 2 + 2 * m)
                    step(dve.tensor_tensor(
                        blockd, ps[:, 2, 64 * m:64 * m + 64].unsqueeze(1).broadcast_to([P, H, 64]),
                        c("own_head").unsqueeze(2).broadcast_to([P, H, 64]), ALU.mult))
                    dve.wait_ge(prep_pe, 3 + 2 * m)
                    step(dve.tensor_copy(w_lat[:, m].rearrange("p h l -> p (h l)"),
                                         ps[:, 3:5, :].rearrange("p a b -> p (a b)")))
                    step(dve.tensor_copy(b_lat[:, m, :], ps[:, 5, 0:H // 2]))
                for r in range(3):
                    step(dve.tensor_copy(w_m2q[:, r * LAT:(r + 1) * LAT], ps[:, 2, 128:160]))
                step(dve.tensor_tensor(
                    bcast[:, 0, :].rearrange("p (h i) -> p h i", h=H),
                    ps[:, 2, 160:168].unsqueeze(1).broadcast_to([P, H, HD]),
                    c("own_head").unsqueeze(2).broadcast_to([P, H, HD]), ALU.mult))
                step(dve.tensor_tensor(cvec[:], ps[:, 2, 168:169], small[:, 65:66], ALU.add))
                step(dve.tensor_copy(bcast[:, 1, :], cvec[:, 0:1].broadcast_to([P, P])))
                dve.wait_ge(prep_pe, 6)
                step(dve.tensor_copy(w_o[:, 0, :], ps[:, 0, 0:P]))
                step(dve.tensor_copy(tmp[:, 3, :], small[:, 2:3].broadcast_to([P, P])))
                dve.wait_ge(prep_pe, 7)
                step(dve.tensor_tensor(bias_lat[:], ps[:, 1, 0:P], rows[:, 5, :], ALU.add))
                dve.wait_ge(we1_high, 1)
                step(dve.tensor_tensor(we1_parts[:, 1].rearrange("p e n -> p (e n)"), we1_raw,
                                       we1_parts[:, 0].rearrange("p e n -> p (e n)").bitcast(F32), ALU.subtract))

            @block.tensor
            def _(pe):
                ident = c("ident")
                pe.wait_ge(prep_dve, 2)
                pe.wait_ge(loaded, n_loads[loaded])
                pe.wait_ge(loaded_small, n_loads[loaded_small])
                pe.transpose(ps[:, 0, 0:P], raw[:, 2, :], ident)
                pe.transpose(ps[:, 0, P:2 * P], raw[:, 3, :], ident)
                pe.transpose(ps[:, 0, 2 * P:3 * P], raw[:, 4, :], ident)
                pe.transpose(ps[:, 0, 3 * P:4 * P], raw[:, 5, :], ident)
                pe.transpose(ps[:, 1, 0:P], raw[:, 6, :], ident)
                pe.transpose(ps[:, 1, P:2 * P], raw[:, 7, :], ident).then_inc(prep_pe, 1)
                pe.wait_ge(prep_dve, PREP_REP)
                pe.matmul(ps[:, 2, 0:64], tmp[0:LAT, 0, :], c("eye_rot")[0:LAT], start=True, stop=True,
                          skip_group_check=True)
                pe.matmul(ps[:, 2, 64:128], tmp[0:LAT, 1, :], c("eye_rot")[0:LAT], start=True, stop=True,
                          skip_group_check=True)
                pe.matmul(ps[:, 2, 128:160], c("eye4")[0:LAT], small[0:LAT, 32:64], start=True, stop=True,
                          skip_group_check=True)
                pe.matmul(ps[:, 2, 160:168], tmp[0:LAT, 2, :], small[0:LAT, 12:20], start=True, stop=True,
                          skip_group_check=True)
                pe.matmul(ps[:, 2, 168:169], tmp[0:LAT, 2, :], small[0:LAT, 21:22], start=True, stop=True,
                          skip_group_check=True).then_inc(prep_pe, 1)
                for m in range(2):
                    pe.wait_ge(prep_dve, PREP_BLOCKD + 3 * m)
                    bd = blockd.rearrange("p h l -> p (h l)")
                    for half in range(2):
                        pe.matmul(ps[:, 3 + half, :], raw[:, m, :], bd[:, half * T:(half + 1) * T],
                                  start=True, stop=True)
                    for pair in range(H // 2):
                        pe.matmul(ps[:, 5, pair:pair + 1], bd[:, pair * P:(pair + 1) * P], small[:, m:m + 1],
                                  start=True, stop=False, skip_group_check=True)
                        ins = pe.matmul(ps[:, 5, pair:pair + 1], c("eye_rot2")[0:LAT],
                                        small[0:LAT, 20 + m:21 + m], start=False, stop=True,
                                        skip_group_check=True)
                    ins.then_inc(prep_pe, 1)
                    if m == 0:
                        pe.matmul(ps[:, 2, 192:256], tmp[0:LAT, 1, :], c("eye_rot")[0:LAT], start=True,
                                  stop=True).then_inc(prep_pe, 1)
                pe.wait_ge(prep_dve, PREP_OUT)
                pe.matmul(ps[:, 0, 0:P], bcast[:, 0, :], cprojT[:], start=True, stop=True).then_inc(prep_pe, 1)
                pe.wait_ge(prep_dve, PREP_OUT + 2)
                pe.matmul(ps[:, 1, 0:P], bcast[:, 1, :], cprojT[:], start=True, stop=False)
                pe.matmul(ps[:, 1, 0:P], tmp[:, 3, :], w_o[:, 0, :], start=False, stop=True).then_inc(prep_pe, 1)

        x_in = sem("x_in")
        misc_full = sem("misc_full")
        misc_done = sem("misc_done")
        st_full = sem("st_full")
        st_done = sem("st_done")
        sm_full = sem("sm_full")
        sm_done = sem("sm_done")
        av_done = sem("av_done")
        o_copied = sem("o_copied")
        parts = sem("parts")
        normed = sem("normed")
        spread = sem("spread")
        folded = sem("folded")
        shifted = sem("shifted")
        z_ready = sem("z_ready")
        z_high = sem("z_high")
        z_low = sem("z_low")
        logits = sem("logits")
        exped = sem("exped")
        gdiff = sem("gdiff")
        gated = sem("gated")
        var_ready = sem("var_ready")
        rstd_ready = sem("rstd_ready")
        dve_step = sem("dve_step")
        zeroed = sem("zeroed")
        seq_done = sem("seq_done")
        stored = sem("stored")
        turn_sems = [x_in, misc_full, misc_done, st_full, st_done, sm_full, sm_done, av_done, o_copied,
                     parts, spread, normed, folded, shifted, z_ready, z_high, z_low, logits, exped, gdiff, gated, var_ready,
                     rstd_ready, dve_step, zeroed, seq_done, stored]

        xv = x.rearrange("(n s) (t p) d -> n s p t d", p=P, s=2)
        ov = out.rearrange("(n s) (t p) d -> n s p t d", p=P, s=2)
        LAST = len(LAYERS) - 1
        count, read = PLAN.count, PLAN.read

        def bank_of(*name):
            return ps[:, PLAN.bank[name], :]

        def queries(s, L, g, j):
            if LAYERS[L] == "latent":
                return q_lat[:, g % 2, j, :]
            return q_x[:, g % 2, :] if s == 0 else q_lat[:, g % 2, 0, :]

        def sums_bank(s, L, g):
            return bank_of("av", s, L, g, QT - 1)

        def z_part(s, L, n):
            return queries(s, L, 0, 0) if n else k_all[:, s]

        def keys(s, L, g, j):
            return k_ops[:, 1 if LAYERS[L] == "latent" else s, g % 2, j, :]

        with nc.Fori(0, x.shape[0] // 2) as b:
            with nc.Block() as block:

                @block.sync
                def _(sp):
                    for s in range(2):
                        sp.dma_start(xs[:, s], xv[b, s]).then_inc(x_in, 16)
                    ends = [n for n in PLAN.order["dve"] if n[0] == "end" and n[2] == LAST]
                    for k, name in enumerate(ends):
                        sp.wait_ge(seq_done, k + 1)
                        sp.dma_start(ov[b, name[1]], xs[:, name[1]]).then_inc(stored, 16)
                    sp.wait_ge(stored, 32)

                @block.gpsimd
                def _(pool):
                    for name in PLAN.order["pool"]:
                        what, s, L = name[:3]
                        if name in PLAN.n["stats"]:
                            n = count("stats", *name)
                            pool.wait_ge(var_ready, n)
                            pool.tensor_tensor(rstd[:, s], vare[:, s], c("neg_half"), ALU.pow).then_inc(rstd_ready, 1)
                        if what == "zero":
                            pool.wait_ge(st_full, count("scores", "cT", s, L))
                            pool.memset(k_ops[:, 1].bitcast(F32), 0.0).then_inc(zeroed, 1)

                @block.tensor
                def _(pe):
                    ident = c("ident")

                    def open_bank(*name):
                        before = PLAN.bank_before[name]
                        if before and before[1][0] == "zT":
                            pe.wait_ge(z_low, count("z_lows", "split", *before[1][1:]))
                            return bank_of(*name)
                        if before and before[0] == "copies":
                            pe.wait_ge(o_copied, count("copies", *before[1]))
                        elif before and before[0] == "misc":
                            pe.wait_ge(misc_done, PLAN.read(*before[:1], *before[1]))
                        elif before and before[0] == "scores":
                            pe.wait_ge(st_done, PLAN.read(*before[:1], *before[1]))
                        elif before:
                            pe.wait_ge(sm_done, PLAN.read(*before[:1], *before[1]))
                        return bank_of(*name)

                    def turn(src, name):
                        bank = open_bank(*name)
                        for t in range(QT):
                            ins = pe.transpose(bank[:, t * P:(t + 1) * P], src[:, t, :], ident)
                        ins.then_inc(st_full if name in PLAN.n["scores"] else misc_full, 1)

                    def rows_out(lhs, w, name):
                        bank = open_bank(*name)
                        n = w.shape[1]
                        for t in range(QT):
                            ins = pe.matmul(bank[:, t * n:(t + 1) * n], lhs[:, t * P:(t + 1) * P], w,
                                            start=True, stop=True, skip_group_check=True)
                        ins.then_inc(st_full if name in PLAN.n["scores"] else misc_full, 1)

                    def columns_out(w, src, name):
                        bank = open_bank(*name)
                        pe.matmul(bank, w, src, start=True, stop=True).then_inc(misc_full, 1)

                    for name in PLAN.order["pe"]:
                        what, s, L = name[:3]
                        kind = LAYERS[L]
                        wsel = ("latent", "ffn", "causal").index(kind)
                        if what in ("v", "pq", "pk", "m1q", "m1k"):
                            pe.wait_ge(st_done, read("scores", "yT", s, L))
                        if what == "yT":
                            pe.wait_ge(normed, count("applied", "apply", s, L))
                            turn(ys[:, s], name)
                        elif what == "v":
                            rows_out(turned[:, s], w_v[:, wsel, :], name)
                        elif what in ("pq", "pk"):
                            w = wrep[:, (0 if kind == "ffn" else 2) + int(what == "pk"), name[3], :]
                            columns_out(w, turned[:, s], name)
                        elif what in ("m1q", "m1k"):
                            h = GH * name[3] + 2 * name[4]
                            w = w_lat[:, int(what == "m1k"), h:h + 2, :].rearrange("p h l -> p (h l)")
                            columns_out(w, turned[:, s], name)
                        elif what in ("m2q", "m2k"):
                            g, j = name[3:]
                            pe.wait_ge(misc_done, read("misc", "m1" + what[-1], s, L, g, j // 2))
                            lo = 64 * (j % 2)
                            w = w_m2q[:] if what == "m2q" else c("sum3")
                            columns_out(w[lo:lo + 64, :], r1[lo:lo + 64, int(what == "m2k"), :], name)
                        elif what == "max":
                            g, j, qt = name[3:]
                            made = ("m2k", s, L, g, j) if kind == "latent" else ("pk", s, L, g)
                            if kind == "latent":
                                made = max(made, ("m2q", s, L, g, j), key=PLAN.n_read["misc"].get)
                            else:
                                made = max(made, ("pq", s, L, g), key=PLAN.n_read["misc"].get)
                                pe.wait_ge(spread, count("spreads", "spread", s, L, g))
                            pe.wait_ge(misc_done, read("misc", *made))
                            q, k = queries(s, L, g, j), keys(s, L, g, j)
                            if kind == "latent":
                                q, k = q[0:96], k[0:96]
                            bank = open_bank(*name)
                            n = T if kind == "ffn" else (qt + 1) * P
                            if kind != "ffn":
                                pe.matmul(bank[:, n - P:n], ident_bf[:], mask_bf[:, 0, :], start=True,
                                          stop=False, skip_group_check=True)
                            pe.matmul(bank[:, 0:n], q[:, qt * P:(qt + 1) * P], k[:, 0:n],
                                      start=(kind == "ffn"), stop=True, skip_group_check=True)\
                                .then_inc(sm_full, 1)
                        elif what == "mT":
                            pe.wait_ge(folded, count("folds", "fold", s, L, name[3]))
                            turn((mx_lat if kind == "latent" else mx[:, s]).bitcast(F32), name)
                        elif what == "st":
                            g, kt, j = name[3:]
                            if kind == "latent":
                                pe.wait_ge(shifted, count("shifts", "mT", s, L, g))
                            else:
                                pe.wait_ge(misc_done, read("misc", "mT", s, L, g))
                            q, k = queries(s, L, g, j), keys(s, L, g, j)
                            bank = open_bank(*name)
                            lo = 0 if kind == "ffn" else kt * P
                            if kind != "ffn":
                                pe.matmul(bank[:, lo:lo + P], ident_bf[:], mask_bf[:, 1, :], start=True,
                                          stop=False, skip_group_check=True)
                            pe.matmul(bank[:, lo:T], k[:, kt * P:(kt + 1) * P], q[:, lo:T],
                                      start=(kind == "ffn"), stop=True, skip_group_check=True)\
                                .then_inc(st_full, 1)
                        elif what == "av":
                            g, kt = name[3:]
                            pe.wait_ge(st_done, read("scores", "v", s, L))
                            pe.wait_ge(st_done, read("scores", "st", s, L, g, kt, GH - 1))
                            bank = open_bank(*name) if kt == QT - 1 else sums_bank(s, L, g)
                            lo = 0 if kind == "ffn" else kt * P
                            slot = PLAN.slot[name]
                            for j in range(GH):
                                ins = pe.matmul(bank[32 * j:32 * j + 2 * HD, lo:T],
                                                va[:, s, kt, GH * g + j, :], wide[:, slot, j, lo:T],
                                                start=(kt == QT - 1), stop=(kt == 0), skip_group_check=True)
                            ins.then_inc(av_done, 1)
                        elif what == "oT":
                            pe.wait_ge(o_copied, count("copies", "av", s, L, name[3], 0))
                            turn(os_[:, s].rearrange("p (t n) -> p t n", t=QT), name)
                        elif what == "cT":
                            last = max(PLAN.n_read["misc"]["oT", s, L, g] for g in range(NG))
                            pe.wait_ge(misc_done, last + 1)
                            turn(ctxs[:, s], name)
                        elif what == "wo":
                            pe.wait_ge(st_done, read("scores", "cT", s, L))
                            rows_out(turned[:, s], w_o[:, wsel, :], name)
                        elif what == "zT":
                            pe.wait_ge(z_ready, count("zs", "z", s, L))
                            turn(ys[:, s], name)
                        elif what == "rt":
                            pe.wait_ge(st_done, read("scores", "zT", s, L))
                            rows_out(turned[:, s], wr_sb[:], name)
                        elif what == "gT":
                            pe.wait_ge(gated, count("gates", "gate", s, L))
                            bank = open_bank(*name)
                            for t in range(QT):
                                ins = pe.transpose(bank[0:E, t * P:(t + 1) * P], gates[:, s, t, :], ident)
                            ins.then_inc(st_full, 1)
                        elif what == "h":
                            e, ch = name[3:]
                            pe.wait_ge(z_low, count("z_lows", "split", s, L))
                            bank = open_bank(*name)
                            w_high, w_low = (we1_parts[:, n, e, ch * P:(ch + 1) * P] for n in range(2))
                            pe.matmul(bank, w_high, z_part(s, L, 0), start=True, stop=False)
                            pe.matmul(bank, w_high, z_part(s, L, 1), start=False, stop=False)
                            pe.matmul(bank, w_low, z_part(s, L, 0), start=False, stop=True).then_inc(st_full, 1)
                        elif what == "o":
                            e = name[3]
                            pe.wait_ge(st_done, read("scores", "h", s, L, e, FC - 1))
                            bank = open_bank(*name)
                            for t in range(QT):
                                for ch in range(FC):
                                    ins = pe.matmul(bank[:, t * P:(t + 1) * P],
                                                    wide[:, PLAN.slot[name], ch, t * P:(t + 1) * P], we2_sb[:, e, ch, :],
                                                    start=(ch == 0), stop=(ch == FC - 1),
                                                    skip_group_check=True)
                            ins.then_inc(sm_full, 1)
                        elif what == "be2":
                            pe.wait_ge(st_done, read("scores", "gT", s, L))
                            bank = open_bank(*name)
                            for t in range(QT):
                                ins = pe.matmul(bank[:, t * P:(t + 1) * P],
                                                m_rows[32 * s:32 * s + E, t * P:(t + 1) * P],
                                                be2_sb[32 * s:32 * s + E, :], start=True, stop=True,
                                                skip_group_check=True)
                            ins.then_inc(misc_full, 1)

                @block.scalar
                def _(act):
                    def slot_free(*unit):
                        before = PLAN.before[unit]
                        if before and before[0] == "av":
                            act.wait_ge(av_done, count("values", *before))
                        elif before:
                            act.wait_ge(sm_full, count("smax", *before))

                    for name in PLAN.order["act"]:
                        what, s, L = name[:3]
                        kind = LAYERS[L]
                        scale = LAT ** -0.5 if kind == "latent" else HD ** -0.5
                        if what in ("pq", "pk", "m2q", "m2k"):
                            n = PLAN.n["parts"][name]
                            act.wait_ge(misc_full, count("misc", *name))
                            if n >= 2:
                                act.wait_ge(misc_done, read("misc", *list(PLAN.n["parts"])[n - 2]))
                            bank = bank_of(*name)
                            if what == "m2q":
                                ins = act.activation(part[:, n % 2], bank, ACT.Identity, scale=c("lq_low"),
                                                     bias=bq_m2_low[:])
                            else:
                                rows_low = {"pq": "q_low", "pk": "k_low", "m2k": "lk_low"}[what]
                                ins = act.activation(part[:, n % 2], bank, ACT.Copy, scale=c(rows_low))
                            ins.then_inc(parts, 1)
                        elif what == "st":
                            g, kt, j = name[3:]
                            slot = PLAN.slot["av", s, L, g, kt]
                            if j == 0:
                                slot_free("av", s, L, g, kt)
                            lo = 0 if kind == "ffn" else kt * P
                            act.wait_ge(st_full, count("scores", *name))
                            act.activation(wide[:, slot, j, lo:T], bank_of(*name)[:, lo:T],
                                           ACT.Exp, scale=scale).then_inc(st_done, 1)
                        elif what == "mT":
                            g = name[3]
                            act.wait_ge(misc_done, read("misc", *name))
                            act.copy(q_lat[96:P, g % 2], m_rows[96:P, :].unsqueeze(1).broadcast_to([32, GH, T]))\
                                .then_inc(shifted, 1)
                        elif what in ("yT", "cT", "zT"):
                            act.wait_ge(st_full, count("scores", *name))
                            act.copy(turned[:, s], bank_of(*name)).then_inc(st_done, 1)
                        elif what == "split":
                            act.copy(z_part(s, L, 0), bank_of("zT", s, L)).then_inc(z_high, 1)
                        elif what == "v":
                            act.wait_ge(st_full, count("scores", *name))
                            act.copy(va[:, s, :, :, 0:HD], bank_of(*name).rearrange("p (t h i) -> p t h i", t=QT, h=H))\
                                .then_inc(st_done, 1)
                        elif what == "gT":
                            act.wait_ge(st_full, count("scores", *name))
                            act.copy(m_rows[32 * s:32 * s + E, :], bank_of(*name)[0:E, :]).then_inc(st_done, 1)
                        elif what == "spread":
                            g = name[3]
                            act.wait_ge(misc_done, read("misc", "pk", s, L, g))
                            if g >= 2:
                                act.wait_ge(st_full, count("scores", "st", s, L, g - 2, 0, GH - 1))
                            if name == ("spread", 1, 1, 0):
                                act.wait_ge(zeroed, 1)
                            for j in range(GH):
                                lo, hi = 32 * j, 32 * j + 32
                                ins = act.copy(keys(s, L, g, j)[lo:hi], k_all[lo:hi, s, :].bitcast(F32))
                            ins.then_inc(spread, 1)
                        elif what == "av" and name[4] == 0:
                            g = name[3]
                            act.wait_ge(av_done, count("values", *name))
                            if NG * L + g > 0:
                                pl, pg = divmod(NG * L + g - 1, NG)
                                act.wait_ge(misc_full, count("misc", "oT", s, pl, pg))
                            act.copy(os_[:, s], sums_bank(s, L, g)).then_inc(o_copied, 1)
                        elif what == "rt":
                            act.wait_ge(logits, count("routes", *name))
                            act.activation(lg[:, s, 1], lg[:, s, 0], ACT.Exp).then_inc(exped, 1)
                        elif what == "top":
                            act.wait_ge(gdiff, count("tops", *name))
                            act.activation(r4[:, s, 3], r4[:, s, 2], ACT.Exp).then_inc(exped, 1)
                        elif what == "h":
                            e, ch = name[3:]
                            if ch == 0:
                                slot_free("o", s, L, e)
                            act.wait_ge(st_full, count("scores", *name))
                            act.activation(wide[:, PLAN.slot["o", s, L, e], ch, :],
                                           bank_of(*name), ACT.Gelu,
                                           bias=be1_sb[:, e * FC + ch:e * FC + ch + 1]).then_inc(st_done, 1)

                @block.vector
                def _(dve):
                    n_step = 0

                    def step(ins):
                        nonlocal n_step
                        n_step += 1
                        ins.then_inc(dve_step, 1)
                        dve.wait_ge(dve_step, n_step)

                    def every_tile(row):
                        return row.unsqueeze(1).broadcast_to([P, QT, P])

                    def stats(s, src, eps):
                        for t in range(QT):
                            ins = dve.bn_stats(st6[:, t, :], src[:, t, :])
                        step(ins)
                        for t in range(QT):
                            ins = dve.bn_aggr(mv[:, s, t, :], st6[:, t, :])
                        step(ins)
                        dve.tensor_scalar(vare[:, s], mv[:, s, :, 1], eps, None, ALU.add).then_inc(var_ready, 1)

                    def apply(s, dst, src, name):
                        dve.wait_ge(rstd_ready, count("stats", *name))
                        for t in range(QT):
                            ins = dve.tensor_scalar(dst[:, t, :], src[:, t, :], mv[:, s, t, 0:1],
                                                    rstd[:, s, t:t + 1], ALU.subtract, ALU.mult)
                        return ins

                    def filled(name):
                        dve.wait_ge(misc_full, count("misc", *name))
                        return bank_of(*name)

                    def gained(dst, gain, bias):
                        step(dve.tensor_tensor(dst, dst, every_tile(gain), ALU.mult))
                        return dve.tensor_tensor(dst, dst, every_tile(bias), ALU.add)

                    over = [P, QT, E]

                    dve.wait_ge(x_in, 32)
                    for name in PLAN.order["dve"]:
                        what, s, L = name[:3]
                        kind = LAYERS[L]
                        x_s = xs[:, s]
                        if what == "norm":
                            stats(s, x_s, 1e-5)
                        elif what == "apply":
                            apply(s, ys[:, s], x_s, ("norm", s, L)).then_inc(normed, 1)
                        elif what in ("m1q", "m1k"):
                            m, pair = int(what == "m1k"), 2 * name[3] + name[4]
                            if pair > 0:
                                prev = ("m2" + what[-1], s, L, (pair - 1) // 2, 2 * ((pair - 1) % 2) + 1)
                                dve.wait_ge(misc_full, count("misc", *prev))
                            dve.scalar_tensor_tensor(
                                out=r1[:, m, :], in0=filled(name), scalar=b_lat[:, m, pair:pair + 1],
                                in1=c("cos_sin"), op0=ALU.add, op1=ALU.mult).then_inc(misc_done, 1)
                        elif what in ("pq", "pk", "m2q", "m2k"):
                            add = {"pq": c("zero"), "pk": c("k_one"), "m2q": bq_m2[:],
                                   "m2k": c("lk_one")[:, name[-1] % GH:name[-1] % GH + 1]}[what]
                            bank = filled(name)
                            dve.wait_ge(parts, count("parts", *name))
                            high = part[:, PLAN.n["parts"][name] % 2].bitcast(F32)
                            g, j = name[3], name[-1] % GH
                            if what == "pk":
                                dst = k_all[:, s]
                                if NG * L + g > NG:
                                    pl, pg = divmod(NG * L + g - 1, NG)
                                    dve.wait_ge(spread, count("spreads", "spread", s, pl, pg))
                            else:
                                dst = keys(s, L, g, j) if what == "m2k" else queries(s, L, g, j)
                                if g >= 2:
                                    dve.wait_ge(st_full, count("scores", "st", s, L, g - 2, 0, GH - 1))
                            dve.scalar_tensor_tensor(out=dst, in0=bank, scalar=add, in1=high,
                                                     op0=ALU.add, op1=ALU.subtract).then_inc(misc_done, 1)
                        elif what == "max":
                            g, j, qt = name[3:]
                            n = T if kind == "ffn" else (qt + 1) * P
                            if j == 0 and qt == 0 and NG * L + g > 0:
                                pl, pg = divmod(NG * L + g - 1, NG)
                                dve.wait_ge(folded, count("folds", "fold", s, pl, pg))
                            dve.wait_ge(sm_full, count("smax", *name))
                            dve.tensor_reduce(nmax[:, s, j, qt:qt + 1],
                                              bank_of(*name)[:, 0:n], AX.X, ALU.max,
                                              negate=True).then_inc(sm_done, 1)
                        elif what == "fold":
                            g = name[3]
                            dve.wait_ge(sm_done, read("smax", "max", s, L, g, GH - 1, QT - 1))
                            if kind == "latent":
                                cols = mx_lat[:, :, M_ROW_LAT:M_ROW_LAT + 2 * GH]\
                                    .rearrange("p t (j s) -> p j t s", s=2)
                                high, low = cols[:, :, :, 0], cols[:, :, :, 1]
                            else:
                                cols = mx[:, s].rearrange("p t (j s) -> p j t s", s=32)
                                high, low = cols[:, :, :, M_ROW], cols[:, :, :, M_ROW + 1]
                            if g > 0:
                                dve.wait_ge(misc_full, count("misc", "mT", s, L, g - 1))
                            step(dve.tensor_copy(high, nmax[:, s]))
                            dve.tensor_tensor(low, nmax[:, s], high.bitcast(F32), ALU.subtract)\
                                .then_inc(folded, 1)
                        elif what == "mT":
                            g = name[3]
                            bank = filled(name)
                            if kind == "latent":
                                if g >= 1:
                                    dve.wait_ge(shifted, count("shifts", "mT", s, L, g - 1))
                                dve.tensor_copy(m_rows[96:P, :], bank[96:P, :]).then_inc(misc_done, 1)
                            else:
                                dst = queries(s, L, g, 0)
                                dve.wait_ge(misc_done, read("misc", "pq", s, L, g))
                                dve.tensor_tensor(dst, bank, dst.bitcast(F32), ALU.add).then_inc(misc_done, 1)
                        elif what == "oT":
                            g = name[3]
                            bank = filled(name).rearrange("p (t j s) -> p t j s", t=QT, s=32)
                            if PLAN.n_read["misc"][name]:
                                dve.wait_ge(misc_done, PLAN.n_read["misc"][name])
                            step(dve.reciprocal(rden[:], bank[:, :, :, HD]))
                            dve.tensor_tensor(
                                ctxs[:, s, :, g * 32:(g + 1) * 32].rearrange("p t (j i) -> p t j i", i=HD),
                                bank[:, :, :, 0:HD], rden[:].unsqueeze(3).broadcast_to([P, QT, GH, HD]),
                                ALU.mult).then_inc(misc_done, 1)
                        elif what == "wo":
                            bank = filled(name).rearrange("p (t d) -> p t d", t=QT)
                            old, dst = (ys[:, s], ctxs[:, s]) if kind == "ffn" else (x_s, x_s)
                            dve.tensor_tensor(dst, bank, old, ALU.add).then_inc(misc_done, 1)
                            dve.wait_ge(misc_done, read("misc", *name))
                            if kind == "latent":
                                step(dve.tensor_tensor(x_s, x_s, every_tile(bias_lat[:]), ALU.add))
                            if kind == "ffn":
                                step(dve.tensor_tensor(dst, dst, every_tile(rows[:, 0, :]), ALU.add))
                                stats(s, dst, 1e-6)
                        elif what == "z":
                            step(apply(s, ys[:, s], ctxs[:, s], ("wo", s, L)))
                            gained(ys[:, s], rows[:, 1, :], rows[:, 2, :]).then_inc(z_ready, 1)
                        elif what == "split":
                            dve.wait_ge(z_high, count("z_highs", "split", s, L))
                            high = z_part(s, L, 0).bitcast(F32)
                            dve.tensor_tensor(z_part(s, L, 1), bank_of("zT", s, L), high, ALU.subtract)\
                                .then_inc(z_low, 1)
                        elif what == "rt":
                            bank = filled(name)[:, 0:QT * E].rearrange("p (t e) -> p t e", t=QT)
                            step(dve.tensor_reduce(r4[:, s, 0], bank, AX.X, ALU.max))
                            dve.tensor_tensor(lg[:, s, 0], bank, r4[:, s, 0].unsqueeze(2).broadcast_to(over),
                                              ALU.subtract).then_inc(misc_done, 1)
                            dve.wait_ge(misc_done, read("misc", *name))
                            dve.nop().then_inc(logits, 1)
                        elif what == "top":
                            r, l = r4[:, s], lg[:, s]
                            dve.wait_ge(exped, count("exps", "rt", s, L))
                            step(dve.tensor_reduce(r[:, 1], l[:, 1], AX.X, ALU.add))
                            step(dve.reciprocal(r[:, 1], r[:, 1]))
                            step(dve.tensor_tensor(l[:, 2], l[:, 1], r[:, 1].unsqueeze(2).broadcast_to(over),
                                                   ALU.mult))
                            for t in range(QT):
                                ins = dve.max(l[:, 3, t, :], l[:, 2, t, :])
                            step(ins)
                            for t in range(QT):
                                ins = dve.max_index(lgi[:, s, t, :], l[:, 3, t, :], l[:, 2, t, :])
                            step(ins)
                            dve.tensor_tensor(r[:, 2], l[:, 3, :, 1], l[:, 3, :, 0], ALU.subtract)\
                                .then_inc(gdiff, 1)
                        elif what == "gate":
                            r, l = r4[:, s], lg[:, s]
                            step(dve.tensor_copy(lgf[:], lgi[:, s]))
                            dve.wait_ge(exped, count("exps", "top", s, L))
                            step(dve.tensor_scalar(r[:, 4], r[:, 3], 1.0, None, ALU.add))
                            step(dve.reciprocal(r[:, 4], r[:, 4]))
                            step(dve.tensor_tensor(r[:, 5], r[:, 3], r[:, 4], ALU.mult))
                            which = c("expert").unsqueeze(1).broadcast_to(over)
                            for n in range(2):
                                ins = dve.tensor_tensor(l[:, 3 + n], which,
                                                        lgf[:, :, n:n + 1].broadcast_to(over), ALU.is_equal)
                            step(ins)
                            for n in range(2):
                                ins = dve.tensor_tensor(l[:, 3 + n], l[:, 3 + n],
                                                        r[:, 4 + n].unsqueeze(2).broadcast_to(over), ALU.mult)
                            step(ins)
                            dve.tensor_tensor(gates[:, s], l[:, 3], l[:, 4], ALU.add).then_inc(gated, 1)
                        elif what == "o":
                            e = name[3]
                            if e == 0:
                                dve.wait_ge(gated, count("gates", "gate", s, L))
                            dve.wait_ge(sm_full, count("smax", *name))
                            bank = bank_of(*name).rearrange("p (t d) -> p t d", t=QT)
                            total = ctxs[:, s]
                            for t in range(QT):
                                ins = dve.scalar_tensor_tensor(
                                    out=total[:, t, :], in0=bank[:, t, :], scalar=gates[:, s, t, e:e + 1],
                                    in1=total[:, t, :], op0=ALU.mult, op1=ALU.add)
                            ins.then_inc(sm_done, 1)
                            dve.wait_ge(sm_done, read("smax", *name))
                        elif what == "be2":
                            bank = filled(name).rearrange("p (t d) -> p t d", t=QT)
                            dve.tensor_tensor(ctxs[:, s], bank, ys[:, s], ALU.add).then_inc(misc_done, 1)
                            dve.wait_ge(misc_done, read("misc", *name))
                        elif what == "sum":
                            stats(s, ctxs[:, s], 1e-6)
                        elif what == "end" and kind == "ffn":
                            total = ctxs[:, s]
                            step(apply(s, total, total, ("sum", s, L)))
                            step(gained(total, rows[:, 3, :], rows[:, 4, :]))
                            ins = dve.tensor_tensor(x_s, x_s, total, ALU.add)
                            if L == LAST:
                                ins.then_inc(seq_done, 1)
                            else:
                                step(ins)

            nc.all_engine_barrier()
            for s in turn_sems:
                nc.gpsimd.sem_clear(s)
            nc.all_engine_barrier()


PREP_REP = 8 + 5 + 3 + 6
PREP_BLOCKD = PREP_REP + 2 + 6 + 2 + 1
PREP_OUT = PREP_BLOCKD - 1 + 6 + 3 + 3

_INS = ["L0_attn_a_x", "L0_attn_a_c_attn_w", "L0_attn_a_c_attn_b", "L0_attn_a_q2l_w", "L0_attn_a_q2l_b",
        "L0_attn_a_kv2l_w", "L0_attn_a_kv2l_b", "L0_attn_a_l2o_w", "L0_attn_a_l2o_b", "L0_attn_a_wqk_w",
        "L0_attn_a_wqk_b", "L0_attn_a_cproj_w", "L0_attn_a_cproj_b", "L0_attn_b_w_qkv", "L0_attn_b_w_o",
        "L0_ffn_Wq", "L0_ffn_Wk", "L0_ffn_Wv", "L0_ffn_Wo", "L0_ffn_bo", "L0_ffn_Wr", "L0_ffn_We1",
        "L0_ffn_be1", "L0_ffn_We2", "L0_ffn_be2", "L0_ffn_ln1_g", "L0_ffn_ln1_b", "L0_ffn_ln2_g",
        "L0_ffn_ln2_b"]


def kernel(**inputs):
    import concourse.bacc as bacc
    from concourse.bass_utils import run_bass_kernel_spmd

    nc = bacc.Bacc("TRN2", target_bir_lowering=False, num_devices=1)
    arrays, args = {}, []
    for name in _INS:
        a = np.ascontiguousarray(inputs[name])
        arrays[name + "_dram"] = a
        args.append(nc.dram_tensor(name + "_dram", a.shape, mybir.dt.from_np(a.dtype), kind="ExternalInput").ap())
    arrays["const_dram"] = CONST
    args.append(nc.dram_tensor("const_dram", CONST.shape, F32, kind="ExternalInput").ap())
    args.append(nc.dram_tensor("out_dram", (4, T, P), F32, kind="ExternalOutput").ap())
    hybrid_kernel(nc, *args)
    r = run_bass_kernel_spmd(nc, [arrays], core_ids=[0])
    return r.results[0]["out_dram"]
```
